# Optimizing a Trainium2 kernel written in Bass

```python
import numpy as np
import jax
import jax.numpy as jnp

def _softmax(x, axis=-1):
    return jax.nn.softmax(x, axis=axis)

def _gelu(x):
    return jax.nn.gelu(x, approximate=True)

def _silu(x):
    return jax.nn.silu(x)

def _sigmoid(x):
    return jax.nn.sigmoid(x)

def _layernorm(x, axis=-1, eps=1e-05):
    m = jnp.mean(x, axis=axis, keepdims=True)
    v = jnp.var(x, axis=axis, keepdims=True)
    return (x - m) / jnp.sqrt(v + eps)

def _scatter_add(tgt, idx, src, axis=0):
    return tgt.at[idx].add(src)

def _segment_sum(src, seg, n):
    return jax.ops.segment_sum(src, seg, n)
kernel_name = 'mk_flamingo_gated_d1_seqx_r8_f89d4c'

def setup_inputs(seed: int=0):
    np.random.seed(seed)
    _w = jnp.asarray

    def _rec_inputs():
        import jax
        import jax.numpy as jnp
        _rk = jax.random.key(seed)
        x = 7.22e-05 + 1 * jax.random.normal(jax.random.fold_in(_rk, 1), (8, 256, 128), jnp.float32)
        _lenS = 256 - jax.random.randint(jax.random.fold_in(_rk, 7), (8,), 0, max(1, 256 // 4) + 1, jnp.int32)
        _lenS2 = 64 - jax.random.randint(jax.random.fold_in(_rk, 8), (8,), 0, max(1, 64 // 4) + 1, jnp.int32)
        _ctx_768P = jax.random.normal(jax.random.fold_in(_rk, 11), (8, 16, 96), jnp.float32)
        _ctx_768c = jax.random.dirichlet(jax.random.fold_in(_rk, 511), 0.3 * jnp.ones((16,), jnp.float32), (8, 64))
        _ctx_768t = jnp.einsum('bsk,bkd->bsd', _ctx_768c, _ctx_768P)
        _ctx_768t = _ctx_768t * jax.lax.rsqrt(jnp.mean(jnp.square(_ctx_768t)) + 1e-12) * 0.953939
        ctx_768 = -0.000191848 + 0.999787 * (_ctx_768t + 0.3 * jax.random.normal(jax.random.fold_in(_rk, 611), (8, 64, 96), jnp.float32))
        _validS = jnp.arange(256)[None, :] < _lenS[:, None]
        _validS2 = jnp.arange(64)[None, :] < _lenS2[:, None]
        _causal = jnp.tril(jnp.ones((256, 256), dtype=bool))
        mask_BxS2_bk0 = jnp.logical_not(jnp.broadcast_to(_validS2[:, :], (8, 64)))
        _g = jax.random.normal(jax.random.fold_in(_rk, 9001), (2, 1), jnp.float32)
        _g = jnp.sign(_g) * jnp.maximum(jnp.abs(_g), 1.0) + (_g == 0) * 1.0
        g_xattn = _g[0]
        g_ffn = _g[1]
        return (x, ctx_768, mask_BxS2_bk0, g_xattn, g_ffn)
    x, ctx_768, mask_BxS2_bk0, g_xattn, g_ffn = _rec_inputs()

    def _L0_xattn_setup():
        import jax, jax.numpy as jnp
        import numpy as np
        HEADS = 8
        DIM_HEAD = 64
        QUERY_DIM = 128
        CONTEXT_DIM = 96
        INNER = HEADS * DIM_HEAD
        key = jax.random.key(seed)
        ks = jax.random.split(key, 8)
        b, n, j = (4, 256, 256)
        x = jax.random.normal(ks[0], (b, n, QUERY_DIM), dtype=jnp.float32)
        context = jax.random.normal(ks[1], (b, j, CONTEXT_DIM), dtype=jnp.float32)
        mask = jax.random.randint(ks[2], (b, j), 0, 2).astype(jnp.bool_)
        W_q = jax.random.normal(ks[3], (QUERY_DIM, INNER), dtype=jnp.float32) / np.sqrt(QUERY_DIM)
        W_k = jax.random.normal(ks[4], (CONTEXT_DIM, INNER), dtype=jnp.float32) / np.sqrt(CONTEXT_DIM)
        W_v = jax.random.normal(ks[5], (CONTEXT_DIM, INNER), dtype=jnp.float32) / np.sqrt(CONTEXT_DIM)
        W_o = jax.random.normal(ks[6], (INNER, QUERY_DIM), dtype=jnp.float32) / np.sqrt(INNER)
        b_o = jax.random.normal(ks[7], (QUERY_DIM,), dtype=jnp.float32) * 0.01
        return {'x': x, 'context': context, 'mask': mask, 'W_q': W_q, 'W_k': W_k, 'W_v': W_v, 'W_o': W_o, 'b_o': b_o}
    _L0_xattn_all = _L0_xattn_setup()
    _L0_xattn_in = {k: v for k, v in _L0_xattn_all.items() if k in ('W_q', 'W_k', 'W_v', 'W_o', 'b_o')}
    del _L0_xattn_all

    def _L0_ffn_setup():
        import jax, jax.numpy as jnp
        import numpy as np
        D = 128
        E = 12
        HS = 2 * D
        HR = 3 * D
        TAU = 1.5

        def _geglu(h):
            a, g = jnp.split(h, 2, axis=-1)
            return a * jax.nn.gelu(g, approximate=False)
        key = jax.random.key(seed)
        ks = jax.random.split(key, 12)

        def xavier(k, shape):
            fan_in, fan_out = (shape[-2], shape[-1])
            lim = jnp.sqrt(6.0 / (fan_in + fan_out))
            return jax.random.uniform(k, shape, jnp.float32, -lim, lim)
        x = jax.random.normal(ks[0], (2, 128, D), jnp.float32)
        Ws1 = xavier(ks[1], (D, 2 * HS))
        bs1 = jnp.zeros((2 * HS,), jnp.float32)
        Ws2 = xavier(ks[2], (HS, D))
        bs2 = jnp.zeros((D,), jnp.float32)
        We1 = xavier(ks[3], (E, D, 2 * HR))
        be1 = jnp.zeros((E, 2 * HR), jnp.float32)
        We2 = xavier(ks[4], (E, HR, D))
        be2 = jnp.zeros((E, D), jnp.float32)
        Wr = xavier(ks[5], (D, E))
        br = jnp.zeros((E,), jnp.float32)
        return {'x': x, 'Ws1': Ws1, 'bs1': bs1, 'Ws2': Ws2, 'bs2': bs2, 'We1': We1, 'be1': be1, 'We2': We2, 'be2': be2, 'Wr': Wr, 'br': br}
    _L0_ffn_all = _L0_ffn_setup()
    _L0_ffn_in = {k: v for k, v in _L0_ffn_all.items() if k in ('Ws1', 'bs1', 'Ws2', 'bs2', 'We1', 'be1', 'We2', 'be2', 'Wr', 'br')}
    del _L0_ffn_all
    return {'x': x, 'ctx_768': ctx_768, 'mask_BxS2_bk0': mask_BxS2_bk0, 'g_xattn': g_xattn, 'g_ffn': g_ffn, 'L0_xattn_W_q': _L0_xattn_in['W_q'], 'L0_xattn_W_k': _L0_xattn_in['W_k'], 'L0_xattn_W_v': _L0_xattn_in['W_v'], 'L0_xattn_W_o': _L0_xattn_in['W_o'], 'L0_xattn_b_o': _L0_xattn_in['b_o'], 'L0_ffn_Ws1': _L0_ffn_in['Ws1'], 'L0_ffn_bs1': _L0_ffn_in['bs1'], 'L0_ffn_Ws2': _L0_ffn_in['Ws2'], 'L0_ffn_bs2': _L0_ffn_in['bs2'], 'L0_ffn_We1': _L0_ffn_in['We1'], 'L0_ffn_be1': _L0_ffn_in['be1'], 'L0_ffn_We2': _L0_ffn_in['We2'], 'L0_ffn_be2': _L0_ffn_in['be2'], 'L0_ffn_Wr': _L0_ffn_in['Wr'], 'L0_ffn_br': _L0_ffn_in['br']}

def reference(x, ctx_768, mask_BxS2_bk0, g_xattn, g_ffn, L0_xattn_W_q, L0_xattn_W_k, L0_xattn_W_v, L0_xattn_W_o, L0_xattn_b_o, L0_ffn_Ws1, L0_ffn_bs1, L0_ffn_Ws2, L0_ffn_bs2, L0_ffn_We1, L0_ffn_be1, L0_ffn_We2, L0_ffn_be2, L0_ffn_Wr, L0_ffn_br):
    import jax
    import jax.numpy as jnp

    def _L0_xattn_ref(x, context, mask, W_q, W_k, W_v, W_o, b_o):
        import jax, jax.numpy as jnp
        import numpy as np
        HEADS = 8
        DIM_HEAD = 64
        QUERY_DIM = 128
        CONTEXT_DIM = 96
        INNER = HEADS * DIM_HEAD
        b, n, _ = x.shape
        j = context.shape[1]
        scale = DIM_HEAD ** (-0.5)
        q = (x @ W_q).reshape(b, n, HEADS, DIM_HEAD)
        k = (context @ W_k).reshape(b, j, HEADS, DIM_HEAD)
        v = (context @ W_v).reshape(b, j, HEADS, DIM_HEAD)
        sim = jnp.einsum('bihd,bjhd->bhij', q, k) * scale
        max_neg = -jnp.finfo(sim.dtype).max
        sim = jnp.where(mask[:, None, None, :], sim, max_neg)
        attn = jax.nn.softmax(sim, axis=-1)
        out = jnp.einsum('bhij,bjhd->bihd', attn, v).reshape(b, n, INNER)
        return out @ W_o + b_o

    def _L0_ffn_ref(x, Ws1, bs1, Ws2, bs2, We1, be1, We2, be2, Wr, br):
        import jax, jax.numpy as jnp
        import numpy as np
        D = 128
        E = 12
        HS = 2 * D
        HR = 3 * D
        TAU = 1.5

        def _geglu(h):
            a, g = jnp.split(h, 2, axis=-1)
            return a * jax.nn.gelu(g, approximate=False)
        B, T, Dm = x.shape
        xf = x.reshape(-1, Dm)
        ys = _geglu(xf @ Ws1 + bs1) @ Ws2 + bs2
        logits = (xf @ Wr + br) / TAU
        top_val, top_idx = jax.lax.top_k(logits, 2)
        top_w = jax.nn.softmax(top_val, axis=-1)
        onehot = jax.nn.one_hot(top_idx, E, dtype=x.dtype)
        w = jnp.einsum('nke,nk->ne', onehot, top_w)
        h = jnp.einsum('nd,edh->enh', xf, We1) + be1[:, None, :]
        act = _geglu(h)
        yE = jnp.einsum('enh,ehd->end', act, We2) + be2[:, None, :]
        yr = jnp.einsum('end,ne->nd', yE, w)
        return (ys + yr).reshape(B, T, Dm)
    x = x + jnp.tanh(g_xattn[0]) * _L0_xattn_ref(_layernorm(x, axis=-1), ctx_768, mask_BxS2_bk0, L0_xattn_W_q, L0_xattn_W_k, L0_xattn_W_v, L0_xattn_W_o, L0_xattn_b_o)
    x = x + jnp.tanh(g_ffn[0]) * _L0_ffn_ref(_layernorm(x, axis=-1), L0_ffn_Ws1, L0_ffn_bs1, L0_ffn_Ws2, L0_ffn_bs2, L0_ffn_We1, L0_ffn_be1, L0_ffn_We2, L0_ffn_be2, L0_ffn_Wr, L0_ffn_br)
    return x

_drawn_inputs = setup_inputs


def setup_inputs(seed=0):
    import zlib

    import numpy as np

    out = dict(_drawn_inputs(seed))
    spreads = {'L0_ffn_bs1': (0.0, 0.1),
     'L0_ffn_bs2': (0.0, 0.1),
     'L0_ffn_be1': (0.0, 0.1),
     'L0_ffn_be2': (0.0, 0.1),
     'L0_ffn_br': (0.0, 0.1)}
    factors = {'L0_xattn_b_o': 4.868}
    for name, (base, spread) in spreads.items():
        noise = np.random.default_rng([zlib.crc32(name.encode()), seed]).standard_normal(out[name].shape)
        drawn = base * np.exp(spread * noise) if base else spread * noise
        out[name] = jnp.asarray(drawn.astype(out[name].dtype))
    for name, factor in factors.items():
        out[name] = (out[name] * factor).astype(out[name].dtype)
    return out
```

```python
from contextlib import ExitStack

import concourse.bass as bass
from concourse import mybir

F32 = mybir.dt.float32
BF16 = mybir.dt.bfloat16
I32 = mybir.dt.int32
U32 = mybir.dt.uint32
U8 = mybir.dt.uint8
ALU = mybir.AluOpType
ACT = mybir.ActivationFunctionType
AX = mybir.AxisListType

P = 128
HEADS = 8
DH = 64
TAU = 1.5
EPS = 1e-5
MASKED = -float(2 ** 120)
NOWHERE = 1 << 20


def flamingo_block(nc, x, ctx, mask, g_xattn, g_ffn, Wq, Wk, Wv, Wo, bo,
                   Ws1, bs1, Ws2, bs2, We1, be1, We2, be2, Wr, br, out):
    B, T, D = x.shape
    KEYS, C = ctx.shape[1:]
    E, _, HE = We1.shape
    HS = Ws1.shape[1]
    HR, HSH = HE // 2, HS // 2
    RC = HR // P
    SC = HSH // P
    TOKENS = B * T
    J = T // P
    NT = B * J
    CAP = TOKENS + P
    ROW = D + 2
    TILES = (2 * TOKENS + E * (P - 1)) // P
    assert D == P and T % P == 0 and HEADS * DH == Wq.shape[1] and HEADS * KEYS == 512
    assert J == 2 and SC == 2 and TILES % 4 == 3 and B % 2 == 0

    slots = nc.dram_tensor("slots", [E * CAP + P, ROW], F32).ap()
    bias_dram = nc.dram_tensor("bias_dram", [E, 3, HE + D], BF16).ap()
    chosen = nc.dram_tensor("chosen", [2 * TOKENS, D], F32).ap()

    with ExitStack() as stack:
        def sb(name, shape, dt=F32):
            return stack.enter_context(nc.sbuf_tensor(name, shape, dt))

        def sem(name):
            return stack.enter_context(nc.semaphore(name))

        bank = [stack.enter_context(nc.psum_tensor(f"bank{i}", [P, 512], F32)) for i in range(8)]

        x_sb = sb("x_sb", [P, B + 1, J, D])
        ctx_sb = sb("ctx_sb", [P, B * KEYS // P, C])
        wq_sb = sb("wq_sb", [P, 4, P])
        wk_sb = sb("wk_sb", [C, 4, P])
        wv_sb = sb("wv_sb", [C, 4, P])
        wo_sb = sb("wo_sb", [P, 4, D])
        mask_sb = sb("mask_sb", [1, B, KEYS], U8)
        mask_add = sb("mask_add", [P, B, KEYS], BF16)
        bo_sb = sb("bo_sb", [P, D])
        bs2_sb = sb("bs2_sb", [P, D])
        br_sb = sb("br_sb", [P, E])
        bs1_sb = sb("bs1_sb", [P, 4])
        gates = sb("gates", [P, 2])
        tg = sb("tg", [P, 2])
        wr_sb = sb("wr_sb", [P, E])
        ws1_sb = sb("ws1_sb", [P, HS])
        ws2_sb = sb("ws2_sb", [P, SC, D])
        we1_sb = sb("we1_sb", [P, E, HE])
        we2_sb = sb("we2_sb", [P, E, RC, D])
        b2_raw = sb("b2_raw", [E, D])
        b1_3 = sb("b1_3", [P, E, HE], BF16)
        b2_3 = sb("b2_3", [P, E, D], BF16)
        b_parts = sb("b_parts", [E, 3, HE + D], BF16)

        ident = sb("ident", [P, P])
        before = sb("before", [P, P], BF16)
        ones_b = sb("ones_b", [P, P], BF16)
        one_row = sb("one_row", [P, P], BF16)
        three_rows = sb("three_rows", [P, P], BF16)
        iota_e = sb("iota_e", [P, E])
        base_e = sb("base_e", [P, E])
        eps_c = sb("eps_c", [P, 1])
        pad_row = sb("pad_row", [P, ROW])
        dest_i = sb("dest_i", [P, B, J, 2], I32)

        m_sb = sb("m_sb", [P, B, HEADS, KEYS])
        vw_sb = sb("vw_sb", [P, B, 4, D])

        st1 = sb("st1", [P, NT + J, 6])
        mv1 = sb("mv1", [P, B + 1, J, 2])
        sd1 = sb("sd1", [P, B + 1, J])
        rs1 = sb("rs1", [P, B + 1, J])
        xn = sb("xn", [P, 2, J, D])
        xb = sb("xb", [P, B, J, D])
        res = xb
        x1 = sb("x1", [P, 2, J, D])
        xnT = sb("xnT", [P, 2, J * P])
        x2T = sb("x2T", [P, B, J * P])
        x2T_now = sb("x2T_now", [P, 2, J * P])
        ln2r = sb("ln2r", [P, J])
        smax = sb("smax", [P, 2, J, HEADS])
        ssum = sb("ssum", [P, 2, J, HEADS])
        srec = sb("srec", [P, 2, J, HEADS])
        shifted = sb("shifted", [P, J, 512])
        ex = sb("ex", [P, J, 512])
        pr = sb("pr", [P, J, 512])
        prT = sb("prT", [P, J, 4, P])
        flat = [b[:, :, :].rearrange("p j n -> p (j n)") for b in (shifted, ex, pr)]
        flat.append(prT[:, :, :, :].rearrange("p j c n -> p (j c n)"))
        wqT = flat[0][:, 0:4 * P].rearrange("p (c n) -> p c n", c=4)
        wkT = flat[0][:, 4 * P:4 * (P + C)].rearrange("p (c n) -> p c n", c=4)
        a_sb = flat[1][0:C, :].rearrange("p (q c n) -> p q c n", q=2, c=4)
        bvo_sb = flat[2][0:C, :].rearrange("p (q c n) -> p q c n", q=2, c=4)
        wvT = flat[3][:, 0:4 * C].rearrange("p (c n) -> p c n", c=4)
        ctxT = flat[3][0:C, 4 * C:4 * C + B * KEYS]
        st2 = sb("st2", [P, J, 6])
        mv2 = sb("mv2", [P, J, 2])
        ln2 = sb("ln2", [P, J])
        y2 = sb("y2", [P, J])
        q2 = sb("q2", [P, J])
        rs2 = sb("rs2", [P, 2, J])
        payload = sb("payload", [P, 2, J, 2, ROW])
        lg = sb("lg", [P, J, E])
        top = sb("top", [P, J, 8])
        topi = sb("topi", [P, J, 8], U32)
        topf = sb("topf", [P, J, 2])
        gd = sb("gd", [P, J])
        ge = sb("ge", [P, J])
        gz = sb("gz", [P, J])
        gr = sb("gr", [P, J])
        oh = sb("oh", [P, J, 2, E])
        hot = sb("hot", [P, 2, J, E], BF16)
        seen = sb("seen", [P, B + 1, E], BF16)
        seen_j = sb("seen_j", [P, E], BF16)
        pb = sb("pb", [P, J, E])
        sl = sb("sl", [P, J, 2, E])
        slot_f = sb("slot_f", [P, J, 2])
        slot_i = sb("slot_i", [P, 2, J, 2], U32)

        cnt = sb("cnt", [1, E])
        pad_f = sb("pad_f", [1, E])
        pad_i = sb("pad_i", [1, E], I32)
        cnt_i = sb("cnt_i", [1, 2, E], I32)
        til = sb("til", [1, E])
        tri_e = sb("tri_e", [1, E, E])
        tt = sb("tt", [1, E, E])
        cum = sb("cum", [1, E])
        coef = sb("coef", [1, E])
        tile_no = sb("tile_no", [1, TILES])
        exp_f = sb("exp_f", [1, TILES])
        exp_i = sb("exp_i", [1, TILES], I32)
        row_s = sb("row_s", [1, TILES])
        row_f = sb("row_f", [1, TILES])
        row_i = sb("row_i", [1, TILES], I32)

        tok = sb("tok", [P, 4, ROW])
        tokT = sb("tokT", [P, 2, P])
        hidT = sb("hidT", [P, 2, HR])
        b1_raw = hidT[0:E, :, :].rearrange("p a n -> p (a n)")
        work = sb("work", [P, 2 * (HE + D)])
        b_rest = work[0:E, :].rearrange("p (a n) -> p a n", a=2)
        gel = work[:, 0:1024].rearrange("p (a n) -> p a n", a=2)
        hid = work[:, 1024:1024 + 2 * HR].rearrange("p (a n) -> p a n", a=2)
        hid_s = ex
        ind = shifted[0:1, :, :].rearrange("p j n -> p (j n)")[:, 0:TILES * E].rearrange("p (t e) -> p t e", e=E)
        indc = pr[0:1, :, :].rearrange("p j n -> p (j n)")[:, 0:TILES * E].rearrange("p (t e) -> p t e", e=E)
        meta = sb("meta", [P, 4, 2])
        yt = sb("yt", [P, 4, D])
        ych = m_sb[:, :, :, :].rearrange("p b h (q k) -> p b (h q k)", q=1).rearrange(
            "p b (j k d) -> p b j k d", j=J, k=2)
        fin = vw_sb[:, 0:B // 2, :, :].rearrange("p b c d -> p (b c d)").rearrange("p (b j d) -> p b j d", b=B, j=J)

        names = """ld_x ld_ctx ld_wq ld_wk ld_wv ld_wo ld_mask ld_bo ld_small ld_wr ld_ws ld_we ld_be
        ld_b3 bias_out consts mask_zero mask_done bias_zero bias_parts bias_rest
        setup_pe setup_act setup_dve fold_pe fold_evac fold_evac_dve x_spare
        st1_done mv1_done sd1_done rs1_done xn_done xb_half xb_done tg_done tg_raw bs2t_done
        xnT_pe xnT_done scores_pe smax_done shifted_done exp_done ssum_done srec_done norm_done
        prT_pe prT_done pv_pe x1_done st2_done mv2_done ln2_done y2_done q2a q2b q2c gz2_done rs2_done x2T_kept pay_x pay_meta
        res0_done x2T_pe x2T_done logits_pe lg_done top_done topi_done topf_done gd_done ge_done
        gz_done gr_done oh_done hot_done seenj_done seen_done pos_pe pb_done sl_done slotf_done slot_done
        cnt_pe cnt_done chain chain_dve apart_dve apart_pool pad_ready table_done pads_stored
        up_pe gel_done hidS_done yS_pe yS_done
        tokT_pe tokT_done meta_done hid_done hidT_pe hidT_done y_pe yt_done
        fin_a fin_done stored""".split()
        S = {n: sem(n) for n in names}
        scat = [sem(f"rows_scattered{i}") for i in range(2)]
        tile_in = [sem(f"tile_loaded{i}") for i in range(4)]
        tile_out = [sem(f"results_scattered{i}") for i in range(4)]
        ych_in = [sem(f"choices_loaded{i}") for i in range(4)]

        def steps(eng, body):
            for s in range(4):
                body(s, s % 2)
            with eng.Fori(2, B // 2) as pair:
                body(pair * 2, 0)
                body(pair * 2 + 1, 1)
            body(B, 0)
            body(B + 1, 1)

        def on(s, lag, count=B):
            return not isinstance(s, int) or 0 <= s - lag < count

        def tile_steps(eng, body):
            for i in range(6):
                body(i, i % 4)
            with eng.Fori(1, (TILES - 3) // 4) as turn:
                for n in range(4):
                    body(turn * 4 + (2 + n), (2 + n) % 4)
            for i in range(TILES - 1, TILES + 2):
                body(i, i % 4)

        def since(eng, s, first, semaphore, count):
            if not isinstance(s, int) or s >= first:
                eng.wait_ge(semaphore, count)

        def apart(eng, *waits):
            for semaphore, count in waits:
                eng.wait_ge(semaphore, count)
            eng.sem_inc(S["apart_dve" if eng is nc.vector else "apart_pool"], 1)

        def pick(t, b):
            if isinstance(b, int):
                return t[:, b]
            v = t[:, bass.ds(b, 1)]
            dims = ["c", "d", "e"][:len(v.shape) - 2]
            return v.rearrange(f"p a {' '.join(dims)} -> p (a {dims[0]}) {' '.join(dims[1:])}")

        block = stack.enter_context(nc.Block())

        @block.sync
        def _(sp):
            xv = x.rearrange("b (p j) d -> p b j d", j=J)
            sp.dma_start(wq_sb[:, :, :], Wq.rearrange("d (c n) -> d c n", c=4)).then_inc(S["ld_wq"], 16)
            sp.dma_start(wk_sb[:, :, :], Wk.rearrange("d (c n) -> d c n", c=4)).then_inc(S["ld_wk"], 16)
            sp.dma_start(ctx_sb[:, :, :], ctx.rearrange("b k c -> (b k) c").rearrange("(t p) c -> p t c", p=P)
                         ).then_inc(S["ld_ctx"], 16)
            sp.dma_start(x_sb[:, 0:B, :, :], xv).then_inc(S["ld_x"], 16)
            sp.dma_start(mask_sb[:, :, :], mask.unsqueeze(0)).then_inc(S["ld_mask"], 16)
            sp.dma_start(wv_sb[:, :, :], Wv.rearrange("d (c n) -> d c n", c=4)).then_inc(S["ld_wv"], 16)
            sp.dma_start(wo_sb[:, :, :], Wo.rearrange("(c p) n -> p c n", p=P)).then_inc(S["ld_wo"], 16)
            for dst, src in ((gates[:, 0:1], g_xattn), (gates[:, 1:2], g_ffn), (bo_sb[:, :], bo), (bs2_sb[:, :], bs2),
                             (br_sb[:, :], br)):
                sp.dma_start(dst, src.partition_broadcast(P)).then_inc(S["ld_small"], 16)
            sp.dma_start(wr_sb[:, :], Wr).then_inc(S["ld_wr"], 16)
            sp.dma_start(b1_raw, be1).then_inc(S["ld_be"], 16)
            sp.dma_start(b2_raw[:, :], be2).then_inc(S["ld_be"], 16)
            with nc.allow_non_contiguous_dma(reason="512 biases, one per partition"):
                sp.dma_start(bs1_sb[:, :], bs1.rearrange("(c p) -> p c", p=P)).then_inc(S["ld_ws"], 16)
            sp.dma_start(ws1_sb[:, :], Ws1).then_inc(S["ld_ws"], 16)
            sp.dma_start(ws2_sb[:, :, :], Ws2.rearrange("(c p) n -> p c n", p=P)).then_inc(S["ld_ws"], 16)
            sp.dma_start(we1_sb[:, :, :], We1.rearrange("e d n -> d e n")).then_inc(S["ld_we"], 16)
            sp.dma_start(we2_sb[:, :, :, :], We2.rearrange("e (c p) n -> p e c n", p=P)).then_inc(S["ld_we"], 16)
            sp.wait_ge(S["bias_zero"], 2)
            sp.wait_ge(S["bias_parts"], 3)
            sp.dma_start(bias_dram, b_parts[:, :, :]).then_inc(S["bias_out"], 16)
            sp.wait_ge(S["bias_out"], 16)
            by_part = bias_dram.rearrange("e t n -> t e n")
            sp.dma_start(b1_3[0:3, :, :], by_part[:, :, 0:HE]).then_inc(S["ld_b3"], 16)
            sp.dma_start(b2_3[0:3, :, :], by_part[:, :, HE:HE + D]).then_inc(S["ld_b3"], 16)

            sp.wait_ge(S["pad_ready"], 1)
            sp.wait_ge(S["consts"], 1)
            with sp.Fori(0, E) as e:
                r = sp.value_load(pad_i[0:1, bass.ds(e, 1)], min_val=0, max_val=E * CAP - P)
                sp.dma_start(slots[bass.ds(r, P), :], pad_row[:, :]).then_inc(S["pads_stored"], 16)
            sp.dma_start(slots[E * CAP:E * CAP + P, :], pad_row[:, :]).then_inc(S["pads_stored"], 16)
            sp.wait_ge(S["pads_stored"], 16 * (E + 1))
            for par in range(2):
                sp.wait_ge(scat[par], 16 * 4 * (B // 2))
            sp.wait_ge(S["table_done"], 2)

            def load(k, u):
                since(sp, k, 4, S["tokT_pe"], k - 3)
                since(sp, k, 4, S["meta_done"], k - 3)
                r = sp.value_load(row_i[0:1, bass.ds(k, 1)], min_val=0, max_val=E * CAP)
                sp.dma_start(tok[:, u, :], slots[bass.ds(r, P), :]).then_inc(tile_in[u], 16)

            for k in range(4):
                load(k, k)
            with sp.Fori(1, TILES // 4) as turn:
                for u in range(4):
                    load(turn * 4 + u, u)
            for k in range(TILES - 3, TILES):
                load(k, k % 4)

            for u in range(4):
                sp.wait_ge(tile_out[u], 16 * ((TILES - u + 3) // 4))
            cv = chosen.rearrange("(b p j k) d -> p b (j k d)", b=B, j=J, k=2)
            for n in range(4):
                w = B // 4
                sp.dma_start(ych[:, n * w:(n + 1) * w, :, :, :].rearrange("p b j k d -> p b (j k d)"),
                             cv[:, n * w:(n + 1) * w, :]).then_inc(ych_in[n], 16)
            ov = out.rearrange("b (p j) d -> p b j d", j=J)
            for n in range(4):
                w = B // 4
                sp.wait_ge(S["fin_done"], n + 1)
                sp.dma_start(ov[:, n * w:(n + 1) * w, :, :], fin[:, n * w:(n + 1) * w, :, :]).then_inc(S["stored"], 16)
            sp.wait_ge(S["stored"], 64)

        @block.gpsimd
        def _(pool):
            g = nc.gpsimd
            g.memset(ident[:, :], 0.0)
            g.memset(before[:, :], 1.0)
            g.memset(pad_row[:, :], 0.0)
            g.memset(one_row[:, :], 0.0)
            g.memset(three_rows[:, :], 0.0)
            g.memset(ones_b[:, :], 1.0)
            g.memset(eps_c[:, :], EPS)
            g.memset(seen[:, 0, :], 0.0)
            g.memset(tri_e[:, :, :], 1.0)
            g.iota(iota_e[:, :], [[1, E]], base=0, channel_multiplier=0, allow_small_or_imprecise_dtypes=True)
            g.iota(base_e[:, :], [[CAP, E]], base=0, channel_multiplier=0, allow_small_or_imprecise_dtypes=True)
            g.iota(tile_no[:, :], [[1, TILES]], base=0, channel_multiplier=0, allow_small_or_imprecise_dtypes=True)
            g.iota(dest_i[:, :, :, :], [[2 * T, B], [2, J], [1, 2]], base=0, channel_multiplier=2 * J
                   ).then_inc(S["chain"], 1)
            pool.wait_ge(S["chain"], 1)
            g.affine_select(out=ident[:, :], in_=ident[:, :], compare_op=ALU.not_equal, fill=1.0, base=0,
                            pattern=[[-1, P]], channel_multiplier=1)
            g.affine_select(out=before[:, :], in_=before[:, :], compare_op=ALU.is_gt, fill=0.0, base=0,
                            pattern=[[1, P]], channel_multiplier=-1)
            g.affine_select(out=tri_e[:, :, :], in_=tri_e[:, :, :], compare_op=ALU.is_ge, fill=0.0, base=0,
                            pattern=[[1, E], [-1, E]], channel_multiplier=0)
            g.memset(one_row[0:1, :], 1.0)
            g.memset(three_rows[0:3, :], 1.0)
            g.iota(pad_row[:, D + 1:D + 2].bitcast(I32), [[0, 1]], base=NOWHERE, channel_multiplier=0
                   ).then_inc(S["consts"], 1)
            g.memset(mask_add[:, :, :], 0.0).then_inc(S["mask_zero"], 1)
            g.memset(b1_3[:, :, :], 0.0).then_inc(S["bias_zero"], 1)
            g.memset(b2_3[:, :, :], 0.0).then_inc(S["bias_zero"], 1)
            pool.wait_ge(S["tg_done"], 1)
            pool.wait_ge(S["ld_small"], 80)
            pool.wait_ge(S["ld_x"], 16)
            g.tensor_scalar(bo_sb[:, :], bo_sb[:, :], tg[:, 0:1], None, ALU.mult).then_inc(S["xb_half"], 1)
            g.tensor_scalar(bs2_sb[:, :], bs2_sb[:, :], tg[:, 1:2], None, ALU.mult).then_inc(S["bs2t_done"], 1)
            pool.wait_ge(S["xb_half"], 1)
            for b in range(B):
                g.tensor_tensor(xb[:, b, :, :], x_sb[:, b, :, :], bo_sb[:, :].unsqueeze(1).to_broadcast([P, J, D]),
                                ALU.add).then_inc(S["xb_done"], 1)
            pool.wait_ge(S["bs2t_done"], 1)

            def step(s, par):
                if on(s, 0):
                    for j in range(J):
                        pool.wait_ge(S["srec_done"], s * J + (j + 1))
                        since(pool, s, 1, S["prT_pe"], s * J + (j - 1))
                        g.tensor_tensor(pr[:, j, :].rearrange("p (h k) -> p h k", h=HEADS),
                                        ex[:, j, :].rearrange("p (h k) -> p h k", h=HEADS),
                                        srec[:, par, j, :].unsqueeze(2).to_broadcast([P, HEADS, KEYS]),
                                        ALU.mult).then_inc(S["norm_done"], 1)
                if on(s, 1):
                    b = s - 1
                    q = 1 - par
                    pool.wait_ge(S["x1_done"], s)
                    g.tensor_tensor(pick(res, b), x1[:, q, :, :], bs2_sb[:, :].unsqueeze(1).to_broadcast([P, J, D]),
                                    ALU.add).then_inc(S["res0_done"], 1)
                    if not isinstance(s, int) or s >= 3:
                        apart(pool, (scat[q], (s - (1 + q)) * (16 * J)))
                    g.tensor_copy(payload[:, q, :, :, D + 1:D + 2].rearrange("p j k o -> p j (k o)").bitcast(I32),
                                  pick(dest_i, b)).then_inc(S["pay_meta"], 1)
                if on(s, 2):
                    b = s - 2
                    apart(pool, (S["slot_done"], s - 1), (S["pay_x"], (s - 1) * J), (S["gr_done"], (s - 1) * 2),
                          (S["pay_meta"], s - 1))
                    for j in range(J):
                        for k in range(2):
                            g.indirect_dma_start(
                                out=slots[:, :],
                                out_offset=bass.IndirectOffsetOnAxis(ap=slot_i[:, par, j, k:k + 1], axis=0),
                                in_=payload[:, par, j, k, :], in_offset=None).then_inc(scat[par], 16)

            steps(pool, step)

            def tile(i, u):
                if on(i, 0, TILES):
                    free = [] if isinstance(i, int) and i < 4 else [(tile_out[u], (i - u) * 4)]
                    apart(pool, (tile_in[u], (i - u) * 4 + 16), *free)
                    g.tensor_copy(meta[:, u, :].bitcast(I32), tok[:, u, D:D + 2].bitcast(I32)
                                  ).then_inc(S["meta_done"], 1)
                if on(i, 2, TILES):
                    v = (u - 2) % 4
                    apart(pool, (S["yt_done"], i - 1), (S["meta_done"], i - 1))
                    g.indirect_dma_start(
                        out=chosen[:, :],
                        out_offset=bass.IndirectOffsetOnAxis(ap=meta[:, v, 1:2].bitcast(U32), axis=0),
                        in_=yt[:, v, :], in_offset=None, bounds_check=2 * TOKENS - 1, oob_is_err=False
                    ).then_inc(tile_out[v], 16)

            tile_steps(pool, tile)

        @block.scalar
        def _(act):
            a = nc.scalar
            act.wait_ge(S["ld_small"], 80)
            a.activation(tg[:, :], gates[:, :], ACT.Tanh).then_inc(S["tg_done"], 1)
            act.wait_ge(S["mv1_done"], NT + J)
            act.wait_ge(S["consts"], 1)
            a.activation(sd1[:, :, :], mv1[:, :, :, 1], ACT.Sqrt, bias=eps_c[:, 0:1]).then_inc(S["sd1_done"], 1)
            act.wait_ge(S["setup_pe"], 2)
            a.activation(wkT, bank[1][:, 0:4 * C].rearrange("p (c n) -> p c n", c=4), ACT.Copy
                         ).then_inc(S["setup_act"], 1)
            act.wait_ge(S["setup_pe"], 4)
            a.activation(wvT, bank[3][:, 0:4 * C].rearrange("p (c n) -> p c n", c=4), ACT.Copy
                         ).then_inc(S["setup_act"], 1)
            act.wait_ge(S["setup_pe"], 6)
            a.activation(a_sb[:, 1, :, :], bank[5][0:C, :].rearrange("p (c n) -> p c n", c=4), ACT.Copy
                         ).then_inc(S["setup_act"], 1)
            act.wait_ge(S["setup_pe"], 8)
            a.activation(bvo_sb[:, 1, :, :], bank[7][0:C, :].rearrange("p (c n) -> p c n", c=4), ACT.Copy
                         ).then_inc(S["setup_act"], 1)
            for h in range(1, HEADS, 2):
                act.wait_ge(S["fold_pe"], h + 1)
                a.activation(m_sb[:, :, h, :], bank[h % 4][:, :].rearrange("p (b k) -> p b k", b=B), ACT.Copy
                             ).then_inc(S["fold_evac"], 1)
            for n in range(1, 8, 2):
                act.wait_ge(S["fold_pe"], HEADS + n + 1)
                for half in range(2):
                    ins = a.activation(vw_sb[64:128, n // 2 * 2 + half, :, :],
                                       bank[4 + n % 4][64 * half:64 * half + 64, :].rearrange("p (c n) -> p c n", c=4),
                                       ACT.Copy)
                ins.then_inc(S["fold_evac"], 1)

            def step(s, par):
                if on(s, 0):
                    act.wait_ge(S["xnT_pe"], s + 1)
                    since(act, s, 2, S["scores_pe"], (s - 1) * J)
                    a.activation(xnT[:, par, :], bank[4][:, 0:J * P], ACT.Copy).then_inc(S["xnT_done"], 1)
                if on(s, 2):
                    act.wait_ge(S["x2T_pe"], s - 1)
                    a.activation(x2T_now[:, par, :], bank[5][:, 0:J * P], ACT.Copy).then_inc(S["x2T_done"], 1)
                    a.activation(pick(x2T, s - 2), bank[5][:, 0:J * P], ACT.Copy).then_inc(S["x2T_kept"], 1)
                if on(s, 1):
                    for j in range(J):
                        act.wait_ge(S["prT_pe"], (s - 1) * J + (j + 1))
                        since(act, s, 2, S["pv_pe"], (s - 1) * J + (j - 1))
                        a.activation(prT[:, j, :, :], bank[2 + j][:, :].rearrange("p (c n) -> p c n", c=4), ACT.Copy
                                     ).then_inc(S["prT_done"], 1)
                if on(s, 0):
                    for j in range(J):
                        act.wait_ge(S["shifted_done"], s * J + (j + 1))
                        since(act, s, 1, S["norm_done"], s * J + (j - 1))
                        a.activation(ex[:, j, :], shifted[:, j, :], ACT.Exp, scale=DH ** -0.5).then_inc(S["exp_done"], 1)
                if on(s, 2):
                    act.wait_ge(S["gd_done"], s - 1)
                    a.activation(ge[:, :], gd[:, :], ACT.Exp, scale=1.0 / TAU).then_inc(S["ge_done"], 1)
                if on(s, 1):
                    act.wait_ge(S["mv2_done"], s * J)
                    a.activation(ln2[:, :], mv2[:, :, 1], ACT.Ln, bias=eps_c[:, 0:1]).then_inc(S["ln2_done"], 1)
                    act.wait_ge(S["ln2_done"], s)
                    a.activation(y2[:, :], ln2[:, :], ACT.Exp, scale=-0.5).then_inc(S["y2_done"], 1)

            steps(act, step)

            for c in range(4):
                for m in range(SC):
                    n = SC * c + m
                    act.wait_ge(S["up_pe"], n + 1)
                    if n >= 2:
                        act.wait_ge(S["hidS_done"], n - 1)
                    a.activation(gel[:, m, :], bank[m][:, :], ACT.Gelu, bias=bs1_sb[:, SC + m:SC + m + 1]
                                 ).then_inc(S["gel_done"], 1)
            U0 = 4 * SC

            def tile(i, u):
                par = u % 2
                if on(i, 0, TILES):
                    act.wait_ge(S["up_pe"], i + (U0 + 1))
                    if isinstance(i, int) and i < 2:
                        act.wait_ge(S["hidS_done"], U0)
                    else:
                        act.wait_ge(S["hid_done"], i - 1)
                    a.activation(gel[:, par, 0:HR], bank[par][:, 0:HR], ACT.Gelu).then_inc(S["gel_done"], 1)
                if on(i, 2, TILES):
                    v = (u - 2) % 4
                    act.wait_ge(S["y_pe"], i - 1)
                    act.wait_ge(S["meta_done"], i - 1)
                    since(act, i, 6, tile_out[v], (i - (2 + v)) * 4)
                    a.activation(yt[:, v, :], bank[4][:, 0:D], ACT.Copy, scale=meta[:, v, 0:1]
                                 ).then_inc(S["yt_done"], 1)

            tile_steps(act, tile)

        @block.vector
        def _(dve):
            v = nc.vector
            v.memset(x_sb[:, B, :, :], 0.0).then_inc(S["x_spare"], 1)
            dve.wait_ge(S["ld_x"], 16)
            dve.wait_ge(S["x_spare"], 1)
            for t in range(NT + J):
                v.bn_stats(st1[:, t, :], x_sb[:, t // J, t % J, :]).then_inc(S["st1_done"], 1)
            dve.wait_ge(S["st1_done"], NT + J)
            for t in range(NT + J):
                v.bn_aggr(mv1[:, t // J, t % J, :], st1[:, t, :]).then_inc(S["mv1_done"], 1)
            dve.wait_ge(S["setup_pe"], 1)
            v.tensor_copy(wqT, bank[0][:, :].rearrange("p (c n) -> p c n", c=4)).then_inc(S["setup_dve"], 1)
            dve.wait_ge(S["setup_pe"], 3)
            v.tensor_copy(ctxT, bank[2][0:C, :]).then_inc(S["setup_dve"], 1)
            dve.wait_ge(S["sd1_done"], 1)
            v.reciprocal(rs1[:, :, :], sd1[:, :, :]).then_inc(S["rs1_done"], 1)
            dve.wait_ge(S["rs1_done"], 1)

            def normalise(b, par):
                since(dve, b, 2, S["xnT_pe"], b - 1)
                for j in range(J):
                    v.tensor_scalar(xn[:, par, j, :], pick(x_sb, b)[:, j, :], pick(mv1, b)[:, j, 0:1],
                                    pick(rs1, b)[:, j:j + 1], ALU.subtract, ALU.mult).then_inc(S["xn_done"], 1)

            normalise(0, 0)
            dve.wait_ge(S["setup_pe"], 5)
            v.tensor_copy(a_sb[:, 0, :, :], bank[4][0:C, :].rearrange("p (c n) -> p c n", c=4)
                          ).then_inc(S["setup_dve"], 1)
            dve.wait_ge(S["setup_pe"], 7)
            v.tensor_copy(bvo_sb[:, 0, :, :], bank[6][0:C, :].rearrange("p (c n) -> p c n", c=4)
                          ).then_inc(S["setup_dve"], 1)
            dve.wait_ge(S["ld_mask"], 16)
            dve.wait_ge(S["mask_zero"], 1)
            v.tensor_scalar(mask_add[0:1, :, :], mask_sb[:, :, :], 0.0, MASKED, ALU.is_equal, ALU.mult).then_inc(S["mask_done"], 1)
            for h in range(0, HEADS, 2):
                dve.wait_ge(S["fold_pe"], h + 1)
                v.tensor_copy(m_sb[:, :, h, :], bank[h % 4][:, :].rearrange("p (b k) -> p b k", b=B)
                              ).then_inc(S["fold_evac_dve"], 1)
            for n in range(0, 8, 2):
                dve.wait_ge(S["fold_pe"], HEADS + n + 1)
                for half in range(2):
                    ins = v.tensor_copy(vw_sb[0:64, n // 2 * 2 + half, :, :],
                                        bank[4 + n % 4][64 * half:64 * half + 64, :].rearrange("p (c n) -> p c n", c=4))
                ins.then_inc(S["fold_evac_dve"], 1)
            dve.wait_ge(S["ld_be"], 32)
            for dst, lo in ((b1_raw, 0), (b2_raw[:, :], HE)):
                w = HE if lo == 0 else D
                v.tensor_copy(b_parts[:, 0, lo:lo + w], dst).then_inc(S["bias_rest"], 1)
            dve.wait_ge(S["bias_rest"], 2)
            for dst, lo in ((b1_raw, 0), (b2_raw[:, :], HE)):
                w = HE if lo == 0 else D
                v.tensor_tensor(b_rest[:, 0, lo:lo + w], dst, b_parts[:, 0, lo:lo + w], ALU.subtract
                                ).then_inc(S["bias_rest"], 1)
            dve.wait_ge(S["bias_rest"], 4)
            v.tensor_copy(b_parts[:, 1, :], b_rest[:, 0, :]).then_inc(S["bias_parts"], 1)
            dve.wait_ge(S["bias_parts"], 1)
            v.tensor_tensor(b_rest[:, 1, :], b_rest[:, 0, :], b_parts[:, 1, :], ALU.subtract).then_inc(S["bias_parts"], 1)
            dve.wait_ge(S["bias_parts"], 2)
            v.tensor_copy(b_parts[:, 2, :], b_rest[:, 1, :]).then_inc(S["bias_parts"], 1)

            def step(s, par):
                if on(s, 2):
                    n = s - 1
                    dve.wait_ge(S["logits_pe"], n)
                    v.tensor_tensor(lg[:, :, :], bank[7][:, 0:J * E].rearrange("p (j e) -> p j e", j=J),
                                    br_sb[:, :].unsqueeze(1).to_broadcast([P, J, E]), ALU.add).then_inc(S["lg_done"], 1)
                    apart(dve, (S["lg_done"], n))
                    for j in range(J):
                        v.max(top[:, j, :], lg[:, j, :]).then_inc(S["top_done"], 1)
                    apart(dve, (S["top_done"], n * J))
                    for j in range(J):
                        v.max_index(topi[:, j, :], top[:, j, :], lg[:, j, :]).then_inc(S["topi_done"], 1)
                    v.tensor_tensor(gd[:, :], top[:, :, 1], top[:, :, 0], ALU.subtract).then_inc(S["gd_done"], 1)
                    dve.wait_ge(S["topi_done"], n * J)
                    v.tensor_copy(topf[:, :, :], topi[:, :, 0:2]).then_inc(S["topf_done"], 1)
                    dve.wait_ge(S["topf_done"], n)
                    v.tensor_tensor(oh[:, :, :, :],
                                    iota_e[:, :].unsqueeze(1).unsqueeze(1).to_broadcast([P, J, 2, E]),
                                    topf[:, :, :].unsqueeze(3).to_broadcast([P, J, 2, E]), ALU.is_equal
                                    ).then_inc(S["oh_done"], 1)
                    dve.wait_ge(S["oh_done"], n)
                    v.tensor_tensor(hot[:, par, :, :], oh[:, :, 0, :], oh[:, :, 1, :], ALU.add).then_inc(S["hot_done"], 1)
                    dve.wait_ge(S["hot_done"], n)
                    v.tensor_tensor(seen_j[:, :], pick(seen, s - 2), hot[:, par, 0, :], ALU.add
                                    ).then_inc(S["seenj_done"], 1)
                    dve.wait_ge(S["seenj_done"], n)
                    v.tensor_tensor(pick(seen, s - 1), seen_j[:, :], hot[:, par, 1, :], ALU.add
                                    ).then_inc(S["seen_done"], 1)
                if on(s, 0):
                    for j in range(J):
                        dve.wait_ge(S["scores_pe"], s * J + (j + 1))
                        sc = bank[j][:, :].rearrange("p (h k) -> p h k", h=HEADS)
                        v.tensor_reduce(smax[:, par, j, :], sc, AX.X, ALU.max).then_inc(S["smax_done"], 1)
                        dve.wait_ge(S["smax_done"], s * J + (j + 1))
                        since(dve, s, 1, S["exp_done"], s * J + (j - 1))
                        v.tensor_tensor(shifted[:, j, :].rearrange("p (h k) -> p h k", h=HEADS), sc,
                                        smax[:, par, j, :].unsqueeze(2).to_broadcast([P, HEADS, KEYS]), ALU.subtract
                                        ).then_inc(S["shifted_done"], 1)
                    for j in range(J):
                        dve.wait_ge(S["exp_done"], s * J + (j + 1))
                        v.tensor_reduce(ssum[:, par, j, :], ex[:, j, :].rearrange("p (h k) -> p h k", h=HEADS),
                                        AX.X, ALU.add).then_inc(S["ssum_done"], 1)
                        dve.wait_ge(S["ssum_done"], s * J + (j + 1))
                        v.reciprocal(srec[:, par, j, :], ssum[:, par, j, :]).then_inc(S["srec_done"], 1)
                if on(s, 1):
                    b = s - 1
                    q = 1 - par
                    dve.wait_ge(S["pv_pe"], s * J)
                    since(dve, s, 3, S["res0_done"], s - 2)
                    if isinstance(s, int) and s == 1:
                        dve.wait_ge(S["xb_done"], B)
                    v.scalar_tensor_tensor(out=x1[:, q, :, :].rearrange("p j d -> p (j d)"), in0=bank[6][:, 0:J * D],
                                           scalar=tg[:, 0:1], in1=pick(xb, b).rearrange("p j d -> p (j d)"),
                                           op0=ALU.mult, op1=ALU.add).then_inc(S["x1_done"], 1)
                    dve.wait_ge(S["x1_done"], s)
                    xv = x1[:, q, :, :]
                    for j in range(J):
                        v.bn_stats(st2[:, j, :], xv[:, j, :]).then_inc(S["st2_done"], 1)
                    apart(dve, (S["st2_done"], s * J))
                    for j in range(J):
                        v.bn_aggr(mv2[:, j, :], st2[:, j, :]).then_inc(S["mv2_done"], 1)
                if on(s, 2):
                    n = s - 1
                    dve.wait_ge(S["ge_done"], n)
                    v.tensor_scalar(gz[:, :], ge[:, :], 1.0, None, ALU.add).then_inc(S["gz_done"], 1)
                    dve.wait_ge(S["gz_done"], n)
                    v.reciprocal(gr[:, :], gz[:, :]).then_inc(S["gz2_done"], 1)
                    dve.wait_ge(S["gz2_done"], n)
                    v.tensor_scalar(payload[:, par, :, 0, D:D + 1].rearrange("p j o -> p (j o)"), gr[:, :], tg[:, 1:2],
                                    None, ALU.mult).then_inc(S["gr_done"], 1)
                    v.scalar_tensor_tensor(out=payload[:, par, :, 1, D:D + 1].rearrange("p j o -> p (j o)"),
                                           in0=gr[:, :], scalar=tg[:, 1:2], in1=ge[:, :], op0=ALU.mult,
                                           op1=ALU.mult).then_inc(S["gr_done"], 1)
                    dve.wait_ge(S["pos_pe"], n)
                    v.tensor_tensor(pb[:, :, :], bank[7][:, 32:32 + J * E].rearrange("p (j e) -> p j e", j=J),
                                    base_e[:, :].unsqueeze(1).to_broadcast([P, J, E]), ALU.add).then_inc(S["pb_done"], 1)
                    dve.wait_ge(S["pb_done"], n)
                    v.tensor_tensor(sl[:, :, :, :], oh[:, :, :, :], pb[:, :, :].unsqueeze(2).to_broadcast([P, J, 2, E]),
                                    ALU.mult).then_inc(S["sl_done"], 1)
                    dve.wait_ge(S["sl_done"], n)
                    v.tensor_reduce(slot_f[:, :, :], sl[:, :, :, :], AX.X, ALU.add).then_inc(S["slotf_done"], 1)
                    dve.wait_ge(S["slotf_done"], n)
                    since(dve, s, 4, scat[par], (s - (2 + par)) * (16 * J))
                    v.tensor_copy(slot_i[:, par, :, :], slot_f[:, :, :]).then_inc(S["slot_done"], 1)
                if on(s, 1):
                    q = 1 - par
                    dve.wait_ge(S["y2_done"], s)
                    v.tensor_tensor(q2[:, :], y2[:, :], y2[:, :], ALU.mult).then_inc(S["q2a"], 1)
                    dve.wait_ge(S["q2a"], s)
                    v.scalar_tensor_tensor(out=rs2[:, 0, :], in0=mv2[:, :, 1], scalar=EPS, in1=q2[:, :], op0=ALU.add,
                                           op1=ALU.mult).then_inc(S["q2b"], 1)
                    dve.wait_ge(S["q2b"], s)
                    v.tensor_scalar(rs2[:, 1, :], rs2[:, 0, :], -0.5, 1.5, ALU.mult, ALU.add).then_inc(S["q2c"], 1)
                    dve.wait_ge(S["q2c"], s)
                    v.tensor_tensor(ln2r[:, :], y2[:, :], rs2[:, 1, :], ALU.mult).then_inc(S["rs2_done"], 1)
                    dve.wait_ge(S["rs2_done"], s)
                    since(dve, s, 3, scat[q], (s - (1 + q)) * (16 * J))
                    for j in range(J):
                        v.tensor_scalar(payload[:, q, j, :, 0:D], xv[:, j, :].unsqueeze(1).to_broadcast([P, 2, D]),
                                        mv2[:, j, 0:1], ln2r[:, j:j + 1], ALU.subtract, ALU.mult
                                        ).then_inc(S["pay_x"], 1)
                if on(s, 0):
                    normalise(s + 1, 1 - par)

            steps(dve, step)

            links = [1]

            def link(ins):
                links[0] += 1
                ins.then_inc(S["chain_dve"], 1)
                dve.wait_ge(S["chain_dve"], links[0] - 1)

            dve.wait_ge(S["cnt_pe"], 1)
            link(v.tensor_copy(cnt[:, :], bank[7][0:1, 64:64 + E]))
            v.tensor_tensor(pad_i[:, :], cnt[:, :], base_e[0:1, :], ALU.add).then_inc(S["pad_ready"], 1)
            link(v.tensor_scalar(til[:, :], cnt[:, :], float(P - 1), None, ALU.add))
            link(v.tensor_copy(cnt_i[:, 0, :], til[:, :]))
            link(v.tensor_scalar(cnt_i[:, 1, :], cnt_i[:, 0, :], 7, None, ALU.logical_shift_right))
            link(v.tensor_copy(til[:, :], cnt_i[:, 1, :]))
            link(v.tensor_tensor(tt[:, :, :], tri_e[:, :, :], til[:, :].unsqueeze(1).to_broadcast([1, E, E]), ALU.mult))
            link(v.tensor_reduce(cum[:, :], tt[:, :, :], AX.X, ALU.add))
            link(v.tensor_scalar(coef[:, :], til[:, :], -float(P), float(CAP), ALU.mult, ALU.add))
            link(v.tensor_tensor(ind[:, :, :], cum[:, :].unsqueeze(1).to_broadcast([1, TILES, E]),
                                 tile_no[:, :].unsqueeze(2).to_broadcast([1, TILES, E]), ALU.is_le))
            link(v.tensor_reduce(exp_f[:, :], ind[:, :, :], AX.X, ALU.add))
            v.tensor_scalar(exp_i[:, :], exp_f[:, :], float(E - 1), None, ALU.min).then_inc(S["table_done"], 1)
            link(v.tensor_tensor(indc[:, :, :], ind[:, :, :], coef[:, :].unsqueeze(1).to_broadcast([1, TILES, E]),
                                 ALU.mult))
            link(v.tensor_reduce(row_s[:, :], indc[:, :, :], AX.X, ALU.add))
            link(v.scalar_tensor_tensor(out=row_f[:, :], in0=tile_no[:, :], scalar=float(P), in1=row_s[:, :],
                                        op0=ALU.mult, op1=ALU.add))
            v.tensor_scalar(row_i[:, :], row_f[:, :], float(E * CAP), None, ALU.min).then_inc(S["table_done"], 1)

            for c in range(4):
                for m in range(SC):
                    n = SC * c + m
                    dve.wait_ge(S["gel_done"], n + 1)
                    if c:
                        dve.wait_ge(S["yS_pe"], c)
                    v.scalar_tensor_tensor(out=hid_s[:, m, :], in0=bank[2 + m][:, :], scalar=bs1_sb[:, m:m + 1],
                                           in1=gel[:, m, :], op0=ALU.add, op1=ALU.mult).then_inc(S["hidS_done"], 1)
                dve.wait_ge(S["yS_pe"], c + 1)
                if c == 0:
                    dve.wait_ge(S["res0_done"], B)
                o = res[:, 2 * c:2 * c + 2, :, :].rearrange("p b j d -> p (b j d)")
                v.scalar_tensor_tensor(out=o, in0=bank[4][:, :], scalar=tg[:, 1:2], in1=o, op0=ALU.mult, op1=ALU.add
                                       ).then_inc(S["yS_done"], 1)
            U0 = 4 * SC

            def turn_tokens(k, par):
                dve.wait_ge(S["tokT_pe"], k + 1)
                dve.wait_ge(S["up_pe"], k + (U0 - 1))
                v.tensor_copy(tokT[:, par, :], bank[7][:, 0:P]).then_inc(S["tokT_done"], 1)

            def tile(i, u):
                par = u % 2
                if on(i, -1, TILES):
                    turn_tokens(i + 1, 1 - par)
                if on(i, 1, TILES):
                    dve.wait_ge(S["hidT_pe"], i)
                    since(dve, i, 3, S["y_pe"], i - 2)
                    v.tensor_copy(hidT[:, 1 - par, :], bank[6 - par][:, 0:HR]).then_inc(S["hidT_done"], 1)
                if on(i, 0, TILES):
                    dve.wait_ge(S["gel_done"], i + (U0 + 1))
                    since(dve, i, 2, S["hidT_pe"], i - 1)
                    v.tensor_tensor(hid[:, par, :], bank[2 + par][:, 0:HR], gel[:, par, 0:HR], ALU.mult
                                    ).then_inc(S["hid_done"], 1)

            turn_tokens(0, 0)
            tile_steps(dve, tile)

            for n in range(4):
                w = B // 4
                r = slice(n * w, (n + 1) * w)
                dve.wait_ge(ych_in[n], 16)
                v.tensor_tensor(fin[:, r, :, :], ych[:, r, :, 0, :], ych[:, r, :, 1, :], ALU.add).then_inc(S["fin_a"], 1)
                dve.wait_ge(S["fin_a"], n + 1)
                v.tensor_tensor(fin[:, r, :, :], fin[:, r, :, :], res[:, r, :, :], ALU.add).then_inc(S["fin_done"], 1)

        @block.tensor
        def _(pe):
            t = nc.tensor
            pe.wait_ge(S["consts"], 1)
            pe.wait_ge(S["ld_wq"], 16)
            for c in range(4):
                ins = t.transpose(bank[0][:, c * P:(c + 1) * P], wq_sb[:, c, :], ident[:, :])
            ins.then_inc(S["setup_pe"], 1)
            pe.wait_ge(S["ld_wk"], 16)
            for c in range(4):
                ins = t.transpose(bank[1][:, c * C:(c + 1) * C], wk_sb[:, c, :], ident[0:C, 0:C])
            ins.then_inc(S["setup_pe"], 1)
            pe.wait_ge(S["ld_ctx"], 16)
            for c in range(4):
                ins = t.transpose(bank[2][0:C, c * P:(c + 1) * P], ctx_sb[:, c, :], ident[:, :])
            ins.then_inc(S["setup_pe"], 1)
            pe.wait_ge(S["ld_wv"], 16)
            for c in range(4):
                ins = t.transpose(bank[3][:, c * C:(c + 1) * C], wv_sb[:, c, :], ident[0:C, 0:C])
            ins.then_inc(S["setup_pe"], 1)
            pe.wait_ge(S["setup_dve"], 1)
            pe.wait_ge(S["setup_act"], 1)
            for q in range(2):
                for c in range(4):
                    ins = t.matmul(bank[4 + q][0:C, c * P:(c + 1) * P], wkT[64 * q:64 * q + 64, c, :],
                                   wqT[64 * q:64 * q + 64, c, :], start=True, stop=True)
                ins.then_inc(S["setup_pe"], 1)
            pe.wait_ge(S["ld_wo"], 16)
            pe.wait_ge(S["setup_act"], 2)
            for q in range(2):
                for c in range(4):
                    ins = t.matmul(bank[6 + q][0:C, c * P:(c + 1) * P], wvT[64 * q:64 * q + 64, c, :],
                                   wo_sb[64 * q:64 * q + 64, c, :], start=True, stop=True)
                ins.then_inc(S["setup_pe"], 1)
            pe.wait_ge(S["setup_dve"], 3)
            pe.wait_ge(S["setup_act"], 3)
            for h in range(HEADS):
                if h >= 4:
                    pe.wait_ge(S["fold_evac_dve"] if h % 2 == 0 else S["fold_evac"], (h - 4) // 2 + 1)
                t.matmul(bank[h % 4][:, :], a_sb[:, h % 2, h // 2, :], ctxT, start=True, stop=True
                         ).then_inc(S["fold_pe"], 1)
            pe.wait_ge(S["setup_dve"], 4)
            pe.wait_ge(S["setup_act"], 4)
            for n in range(8):
                if n >= 4:
                    pe.wait_ge(S["fold_evac_dve"] if n % 2 == 0 else S["fold_evac"], 4 + (n - 4) // 2 + 1)
                t.matmul(bank[4 + n % 4][:, :], ctxT[:, n // 2 * P:(n // 2 + 1) * P],
                         bvo_sb[:, n % 2, :, :].rearrange("p c n -> p (c n)"), start=True, stop=True
                         ).then_inc(S["fold_pe"], 1)
            pe.wait_ge(S["fold_evac_dve"], 8)
            pe.wait_ge(S["fold_evac"], 8)
            pe.wait_ge(S["mask_done"], 1)
            pe.wait_ge(S["ld_wr"], 16)

            def step(s, par):
                if on(s, 0):
                    pe.wait_ge(S["xn_done"], s * J + J)
                    for j in range(J):
                        ins = t.transpose(bank[4][:, j * P:(j + 1) * P], xn[:, par, j, :], ident[:, :])
                    ins.then_inc(S["xnT_pe"], 1)
                if on(s, 2):
                    b = s - 2
                    n = s - 1
                    pe.wait_ge(S["pay_x"], n * J)
                    for j in range(J):
                        ins = t.transpose(bank[5][:, j * P:(j + 1) * P], payload[:, par, j, 0, 0:D], ident[:, :])
                    ins.then_inc(S["x2T_pe"], 1)
                if on(s, 1):
                    for j in range(J):
                        pe.wait_ge(S["norm_done"], (s - 1) * J + (j + 1))
                        for c in range(4):
                            ins = t.transpose(bank[2 + j][:, c * P:(c + 1) * P], pr[:, j, c * P:(c + 1) * P],
                                              ident[:, :])
                        ins.then_inc(S["prT_pe"], 1)
                if on(s, 2):
                    pe.wait_ge(S["x2T_done"], n)
                    since(pe, s, 3, S["pb_done"], n - 1)
                    for j in range(J):
                        ins = t.matmul(bank[7][:, j * E:(j + 1) * E], x2T_now[:, par, j * P:(j + 1) * P], wr_sb[:, :], start=True, stop=True)
                    ins.then_inc(S["logits_pe"], 1)
                if on(s, 0):
                    pe.wait_ge(S["xnT_done"], s + 1)
                    for j in range(J):
                        since(pe, s, 1, S["shifted_done"], s * J + (j - 1))
                        t.matmul(bank[j][:, :], xnT[:, par, j * P:(j + 1) * P],
                                 pick(m_sb, s).rearrange("p h k -> p (h k)"), start=True, stop=False)
                        t.matmul(bank[j][:, :], one_row[:, :], pick(mask_add, s).unsqueeze(1).to_broadcast([P, HEADS, KEYS]), start=False, stop=True
                                 ).then_inc(S["scores_pe"], 1)
                if on(s, 1):
                    vw = pick(vw_sb, s - 1)
                    since(pe, s, 2, S["x1_done"], s - 1)
                    for j in range(J):
                        pe.wait_ge(S["prT_done"], (s - 1) * J + (j + 1))
                        for c in range(4):
                            ins = t.matmul(bank[6][:, j * D:(j + 1) * D], prT[:, j, c, :], vw[:, c, :],
                                           start=(c == 0), stop=(c == 3))
                        ins.then_inc(S["pv_pe"], 1)
                if on(s, 2):
                    pe.wait_ge(S["lg_done"], n)
                    pe.wait_ge(S["hot_done"], n)
                    sv = pick(seen, b)
                    t.matmul(bank[7][:, 32:32 + E], ones_b[:, :], sv, start=True, stop=False)
                    t.matmul(bank[7][:, 32:32 + E], before[:, :], hot[:, par, 0, :], start=False, stop=True)
                    t.matmul(bank[7][:, 32 + E:32 + 2 * E], ones_b[:, :], sv, start=True, stop=False)
                    t.matmul(bank[7][:, 32 + E:32 + 2 * E], ones_b[:, :], hot[:, par, 0, :], start=False, stop=False)
                    t.matmul(bank[7][:, 32 + E:32 + 2 * E], before[:, :], hot[:, par, 1, :], start=False, stop=True
                             ).then_inc(S["pos_pe"], 1)

            steps(pe, step)

            pe.wait_ge(S["seen_done"], B)
            pe.wait_ge(S["pb_done"], B)
            t.matmul(bank[7][:, 64:64 + E], ones_b[:, :], seen[:, B, :], start=True, stop=True).then_inc(S["cnt_pe"], 1)

            pe.wait_ge(S["ld_ws"], 48)
            pe.wait_ge(S["ld_b3"], 32)
            pe.wait_ge(S["x2T_kept"], B)
            pe.wait_ge(S["shifted_done"], NT)
            pe.wait_ge(S["prT_done"], NT)

            def shared_up(c):
                for m in range(SC):
                    n = SC * c + m
                    if n >= 2:
                        pe.wait_ge(S["hidS_done"], n - 1)
                    xt = x2T[:, 2 * c:2 * c + 2, :].rearrange("p b n -> p (b n)")
                    t.matmul(bank[m][:, :], ws1_sb[:, (SC + m) * P:(SC + m + 1) * P], xt, start=True, stop=True)
                    t.matmul(bank[2 + m][:, :], ws1_sb[:, m * P:(m + 1) * P], xt, start=True, stop=True
                             ).then_inc(S["up_pe"], 1)

            shared_up(0)
            for c in range(4):
                if c < 3:
                    shared_up(c + 1)
                pe.wait_ge(S["hidS_done"], SC * (c + 1))
                if c:
                    pe.wait_ge(S["yS_done"], c)
                for n in range(4):
                    for m in range(SC):
                        ins = t.matmul(bank[4][:, n * D:(n + 1) * D], hid_s[:, m, n * P:(n + 1) * P], ws2_sb[:, m, :],
                                       start=(m == 0), stop=(m == SC - 1))
                ins.then_inc(S["yS_pe"], 1)

            U0 = 4 * SC
            pe.wait_ge(S["ld_we"], 32)
            pe.wait_ge(S["table_done"], 2)
            pe.wait_ge(S["yS_done"], 4)
            pe.wait_ge(S["x1_done"], B)
            pe.wait_ge(S["chain_dve"], 1)

            def turn_tokens(k, u):
                pe.wait_ge(tile_in[u], (k - u) * 4 + 16)
                since(pe, k, 1, S["tokT_done"], k)
                t.transpose(bank[7][:, 0:P], tok[:, u, 0:D], ident[:, :]).then_inc(S["tokT_pe"], 1)

            def tile(i, u):
                par = u % 2
                if on(i, -1, TILES):
                    turn_tokens(i + 1, (u + 1) % 4)
                if on(i, 0, TILES):
                    e = pe.value_load(exp_i[0:1, bass.ds(i, 1)], min_val=0, max_val=E - 1)
                    w = pick(we1_sb, e)
                    bias = pick(b1_3, e)
                    pe.wait_ge(S["tokT_done"], i + 1)
                    if isinstance(i, int) and i < 2:
                        pe.wait_ge(S["hidS_done"], U0)
                    else:
                        pe.wait_ge(S["hid_done"], i - 1)
                    t.matmul(bank[par][:, 0:HR], tokT[:, par, :], w[:, HR:HE], start=True, stop=False)
                    t.matmul(bank[par][:, 0:HR], three_rows[:, :], bias[:, HR:HE], start=False, stop=True)
                    t.matmul(bank[2 + par][:, 0:HR], tokT[:, par, :], w[:, 0:HR], start=True, stop=False)
                    t.matmul(bank[2 + par][:, 0:HR], three_rows[:, :], bias[:, 0:HR], start=False, stop=True
                             ).then_inc(S["up_pe"], 1)
                if on(i, 1, TILES):
                    pe.wait_ge(S["hid_done"], i)
                    since(pe, i, 3, S["hidT_done"], i - 2)
                    for c in range(RC):
                        ins = t.transpose(bank[6 - par][:, c * P:(c + 1) * P], hid[:, 1 - par, c * P:(c + 1) * P],
                                          ident[:, :])
                    ins.then_inc(S["hidT_pe"], 1)
                if on(i, 2, TILES):
                    e = pe.value_load(exp_i[0:1, bass.ds(i - 2, 1)], min_val=0, max_val=E - 1)
                    w = pick(we2_sb, e)
                    pe.wait_ge(S["hidT_done"], i - 1)
                    since(pe, i, 3, S["yt_done"], i - 2)
                    for c in range(RC):
                        t.matmul(bank[4][:, 0:D], hidT[:, par, c * P:(c + 1) * P], w[:, c, :], start=(c == 0),
                                 stop=False)
                    t.matmul(bank[4][:, 0:D], three_rows[:, :], pick(b2_3, e), start=False, stop=True
                             ).then_inc(S["y_pe"], 1)

            turn_tokens(0, 0)
            tile_steps(pe, tile)


_INS = ["x", "ctx_768", "mask_BxS2_bk0", "g_xattn", "g_ffn", "L0_xattn_W_q", "L0_xattn_W_k", "L0_xattn_W_v",
        "L0_xattn_W_o", "L0_xattn_b_o", "L0_ffn_Ws1", "L0_ffn_bs1", "L0_ffn_Ws2", "L0_ffn_bs2", "L0_ffn_We1",
        "L0_ffn_be1", "L0_ffn_We2", "L0_ffn_be2", "L0_ffn_Wr", "L0_ffn_br"]


def kernel(**inputs):
    import numpy as np
    import concourse.bacc as bacc
    from concourse.bass_utils import run_bass_kernel_spmd

    nc = bacc.Bacc("TRN2", target_bir_lowering=False, num_devices=1)
    arrays, args = {}, []
    for name in _INS:
        a = np.ascontiguousarray(inputs[name])
        arrays[f"in_{name}"] = a
        args.append(nc.dram_tensor(f"in_{name}", a.shape, mybir.dt.from_np(a.dtype), kind="ExternalInput").ap())
    shape = inputs["x"].shape
    out = nc.dram_tensor("out_dram", shape, F32, kind="ExternalOutput").ap()
    flamingo_block(nc, *args, out)
    return run_bass_kernel_spmd(nc, [arrays], core_ids=[0]).results[0]["out_dram"]
```

```python
from contextlib import ExitStack

import concourse.bass as bass
from concourse import mybir

F32 = mybir.dt.float32
BF16 = mybir.dt.bfloat16
I32 = mybir.dt.int32
U32 = mybir.dt.uint32
U8 = mybir.dt.uint8
ALU = mybir.AluOpType
ACT = mybir.ActivationFunctionType
AX = mybir.AxisListType

P = 128
HEADS = 8
DH = 64
TAU = 1.5
EPS = 1e-5
MASKED = -float(2 ** 120)
NOWHERE = 1 << 20


def flamingo_block(nc, x, ctx, mask, g_xattn, g_ffn, Wq, Wk, Wv, Wo, bo,
                   Ws1, bs1, Ws2, bs2, We1, be1, We2, be2, Wr, br, out):
    B, T, D = x.shape
    KEYS, C = ctx.shape[1:]
    E, _, HE = We1.shape
    HS = Ws1.shape[1]
    HR, HSH = HE // 2, HS // 2
    RC = HR // P
    SC = HSH // P
    TOKENS = B * T
    J = T // P
    NT = B * J
    CAP = TOKENS + P
    ROW = D + 2
    TILES = (2 * TOKENS + E * (P - 1)) // P
    assert D == P and T % P == 0 and HEADS * DH == Wq.shape[1] and HEADS * KEYS == 512
    assert J == 2 and SC == 2 and TILES % 4 == 3 and B % 2 == 0

    slots = nc.dram_tensor("slots", [E * CAP + P, ROW], F32).ap()
    bias_dram = nc.dram_tensor("bias_dram", [E, 3, HE + D], BF16).ap()
    chosen = nc.dram_tensor("chosen", [2 * TOKENS, D], F32).ap()

    with ExitStack() as stack:
        def sb(name, shape, dt=F32):
            return stack.enter_context(nc.sbuf_tensor(name, shape, dt))

        def sem(name):
            return stack.enter_context(nc.semaphore(name))

        bank = [stack.enter_context(nc.psum_tensor(f"bank{i}", [P, 512], F32)) for i in range(8)]

        x_sb = sb("x_sb", [P, B + 2, J, D])
        ctx_sb = sb("ctx_sb", [P, B * KEYS // P, C])
        wq_sb = sb("wq_sb", [P, 4, P])
        wk_sb = sb("wk_sb", [C, 4, P])
        wv_sb = sb("wv_sb", [C, 4, P])
        wo_sb = sb("wo_sb", [P, 4, D])
        mask_sb = sb("mask_sb", [1, B, KEYS], U8)
        mask_add = sb("mask_add", [P, B, KEYS], BF16)
        bo_sb = sb("bo_sb", [P, D])
        bs2_sb = sb("bs2_sb", [P, D])
        br_sb = sb("br_sb", [P, E])
        bs1_sb = sb("bs1_sb", [P, 4])
        gates = sb("gates", [P, 2])
        tg = sb("tg", [P, 2])
        wr_sb = sb("wr_sb", [P, E])
        ws1_sb = sb("ws1_sb", [P, HS])
        ws2_sb = sb("ws2_sb", [P, SC, D])
        we1_sb = sb("we1_sb", [P, E, HE])
        we2_sb = sb("we2_sb", [P, E, RC, D])
        b2_raw = sb("b2_raw", [E, D])
        b1_3 = sb("b1_3", [P, E, HE], BF16)
        b2_3 = sb("b2_3", [P, E, D], BF16)
        b_parts = sb("b_parts", [E, 3, HE + D], BF16)

        ident = sb("ident", [P, P])
        before = sb("before", [P, P], BF16)
        ones_b = sb("ones_b", [P, P], BF16)
        one_row = sb("one_row", [P, P], BF16)
        three_rows = sb("three_rows", [P, P], BF16)
        iota_e = sb("iota_e", [P, E])
        base_e = sb("base_e", [P, E])
        eps_c = sb("eps_c", [P, 1])
        pad_row = sb("pad_row", [P, ROW])
        dest_i = sb("dest_i", [P, B, J, 2], I32)

        m_sb = sb("m_sb", [P, B, HEADS, KEYS])
        vw_sb = sb("vw_sb", [P, B, 4, D])

        st1 = sb("st1", [P, NT, 6])
        mv1 = sb("mv1", [P, B + 2, J, 2])
        sd1 = sb("sd1", [P, B + 2, J])
        rs1 = sb("rs1", [P, B + 2, J])
        nb1 = sb("nb1", [P, B + 2, J])
        xn = sb("xn", [P, 2, J, D])
        xb = sb("xb", [P, B, J, D])
        res = xb
        x1 = sb("x1", [P, 2, J, D])
        xnT = sb("xnT", [P, 2, J * P])
        x2T = sb("x2T", [P, B, J * P])
        x2T_now = sb("x2T_now", [P, 2, J * P])
        ln2r = sb("ln2r", [P, J])
        smax = sb("smax", [P, 2, J, HEADS])
        ssum = sb("ssum", [P, 2, J, HEADS])
        srec = sb("srec", [P, 2, J, HEADS])
        shifted = sb("shifted", [P, J, 512])
        ex = sb("ex", [P, J, 512])
        pr = sb("pr", [P, J, 512])
        prT = sb("prT", [P, J, 4, P])
        flat = [b[:, :, :].rearrange("p j n -> p (j n)") for b in (shifted, ex, pr)]
        flat.append(prT[:, :, :, :].rearrange("p j c n -> p (j c n)"))
        wqT = flat[0][:, 0:4 * P].rearrange("p (c n) -> p c n", c=4)
        wkT = flat[0][:, 4 * P:4 * (P + C)].rearrange("p (c n) -> p c n", c=4)
        a_sb = flat[1][0:C, :].rearrange("p (q c n) -> p q c n", q=2, c=4)
        bvo_sb = flat[2][0:C, :].rearrange("p (q c n) -> p q c n", q=2, c=4)
        wvT = flat[3][:, 0:4 * C].rearrange("p (c n) -> p c n", c=4)
        ctxT = flat[3][0:C, 4 * C:4 * C + B * KEYS]
        st2 = sb("st2", [P, J, 6])
        mv2 = sb("mv2", [P, J, 2])
        ln2 = sb("ln2", [P, J])
        nb2 = sb("nb2", [P, J])
        y2 = sb("y2", [P, J])
        q2 = sb("q2", [P, J])
        rs2 = sb("rs2", [P, 2, J])
        payload = sb("payload", [P, 2, J, 2, ROW])
        lg = sb("lg", [P, J, E])
        top = sb("top", [P, J, 8])
        topi = sb("topi", [P, J, 8], U32)
        topf = sb("topf", [P, J, 2])
        gd = sb("gd", [P, J])
        ge = sb("ge", [P, J])
        gz = sb("gz", [P, J])
        gr = sb("gr", [P, J])
        oh = sb("oh", [P, J, 2, E])
        hot = sb("hot", [P, 2, J, E], BF16)
        seen = sb("seen", [P, B + 1, E], BF16)
        seen_j = sb("seen_j", [P, E], BF16)
        pb = sb("pb", [P, J, E])
        sl = sb("sl", [P, J, 2, E])
        slot_f = sb("slot_f", [P, J, 2])
        slot_i = sb("slot_i", [P, 2, J, 2], U32)

        cnt = sb("cnt", [1, E])
        pad_f = sb("pad_f", [1, E])
        pad_i = sb("pad_i", [1, E], I32)
        cnt_i = sb("cnt_i", [1, 2, E], I32)
        til = sb("til", [1, E])
        tri_e = sb("tri_e", [1, E, E])
        tt = sb("tt", [1, E, E])
        cum = sb("cum", [1, E])
        coef = sb("coef", [1, E])
        tile_no = sb("tile_no", [1, TILES])
        exp_f = sb("exp_f", [1, TILES])
        exp_i = sb("exp_i", [1, TILES], I32)
        row_s = sb("row_s", [1, TILES])
        row_f = sb("row_f", [1, TILES])
        row_i = sb("row_i", [1, TILES], I32)

        tok = sb("tok", [P, 4, ROW])
        tokT = sb("tokT", [P, 2, P])
        hidT = sb("hidT", [P, 2, HR])
        b1_raw = hidT[0:E, :, :].rearrange("p a n -> p (a n)")
        work = sb("work", [P, 2 * (HE + D)])
        b_rest = work[0:E, :].rearrange("p (a n) -> p a n", a=2)
        gel = work[:, 0:1024].rearrange("p (a n) -> p a n", a=2)
        hid = work[:, 1024:1024 + 2 * HR].rearrange("p (a n) -> p a n", a=2)
        hid_s = (ex, prT[:, :, :, :].rearrange("p j c n -> p j (c n)"))
        ind = shifted[0:1, :, :].rearrange("p j n -> p (j n)")[:, 0:TILES * E].rearrange("p (t e) -> p t e", e=E)
        indc = pr[0:1, :, :].rearrange("p j n -> p (j n)")[:, 0:TILES * E].rearrange("p (t e) -> p t e", e=E)
        meta = sb("meta", [P, 4, 2])
        yt = sb("yt", [P, 4, D])
        ych = m_sb[:, :, :, :].rearrange("p b h (q k) -> p b (h q k)", q=1).rearrange(
            "p b (j k d) -> p b j k d", j=J, k=2)
        fin = vw_sb[:, 0:B // 2, :, :].rearrange("p b c d -> p (b c d)").rearrange("p (b j d) -> p b j d", b=B, j=J)

        names = """ld_x ld_ctx ld_wq ld_wk ld_wv ld_wo ld_mask ld_bo ld_small ld_wr ld_ws ld_we ld_be
        ld_b3 bias_out consts mask_zero mask_done bias_zero bias_parts bias_rest
        setup_pe setup_act setup_dve fold_pe fold_evac fold_evac_dve
        st1_done mv1_done sd1_done rs1_done chain_rs1 xn_done xb_half xb_done tg_done tg_raw bs2t_done
        xnT_pe xnT_done scores_pe smax_done shifted_done exp_done ssum_done srec_done norm_done
        prT_pe prT_done pv_pe x1_done st2_done mv2_done ln2_done y2_done q2a q2b q2c q2d gz2_done rs2_done x2T_kept pay_x pay_meta
        res0_done x2T_pe x2T_done logits_pe lg_done top_done topi_done topf_done gd_done ge_done
        gz_done gr_done oh_done hot_done seenj_done seen_done pos_pe pb_done sl_done slotf_done slot_done
        cnt_pe cnt_done chain chain_dve apart_dve apart_pool pad_ready table_done pads_stored
        up_pe gel_done hidS_done yS_pe yS_done
        tokT_pe tokT_done meta_done hid_done hidT_pe hidT_done y_pe yt_done
        fin_a fin_done stored""".split()
        S = {n: sem(n) for n in names}
        scat = [sem(f"rows_scattered{i}") for i in range(2)]
        tile_in = [sem(f"tile_loaded{i}") for i in range(4)]
        tile_out = [sem(f"results_scattered{i}") for i in range(4)]
        ych_in = [sem(f"choices_loaded{i}") for i in range(4)]

        def steps(eng, body):
            for s in range(4):
                body(s, s % 2)
            with eng.Fori(2, B // 2) as pair:
                body(pair * 2, 0)
                body(pair * 2 + 1, 1)
            body(B, 0)
            body(B + 1, 1)

        def on(s, lag, count=B):
            return not isinstance(s, int) or 0 <= s - lag < count

        def tile_steps(eng, body):
            for i in range(6):
                body(i, i % 4)
            with eng.Fori(1, (TILES - 3) // 4) as turn:
                for n in range(4):
                    body(turn * 4 + (2 + n), (2 + n) % 4)
            for i in range(TILES - 1, TILES + 2):
                body(i, i % 4)

        def since(eng, s, first, semaphore, count):
            if not isinstance(s, int) or s >= first:
                eng.wait_ge(semaphore, count)

        def apart(eng, *waits):
            for semaphore, count in waits:
                eng.wait_ge(semaphore, count)
            eng.sem_inc(S["apart_dve" if eng is nc.vector else "apart_pool"], 1)

        def pick(t, b):
            if isinstance(b, int):
                return t[:, b]
            v = t[:, bass.ds(b, 1)]
            dims = ["c", "d", "e"][:len(v.shape) - 2]
            return v.rearrange(f"p a {' '.join(dims)} -> p (a {dims[0]}) {' '.join(dims[1:])}")

        block = stack.enter_context(nc.Block())

        @block.sync
        def _(sp):
            xv = x.rearrange("b (p j) d -> p b j d", j=J)
            sp.dma_start(wq_sb[:, :, :], Wq.rearrange("d (c n) -> d c n", c=4)).then_inc(S["ld_wq"], 16)
            sp.dma_start(wk_sb[:, :, :], Wk.rearrange("d (c n) -> d c n", c=4)).then_inc(S["ld_wk"], 16)
            sp.dma_start(ctx_sb[:, :, :], ctx.rearrange("b k c -> (b k) c").rearrange("(t p) c -> p t c", p=P)
                         ).then_inc(S["ld_ctx"], 16)
            sp.dma_start(x_sb[:, 0:B, :, :], xv).then_inc(S["ld_x"], 16)
            sp.dma_start(mask_sb[:, :, :], mask.unsqueeze(0)).then_inc(S["ld_mask"], 16)
            sp.dma_start(wv_sb[:, :, :], Wv.rearrange("d (c n) -> d c n", c=4)).then_inc(S["ld_wv"], 16)
            sp.dma_start(wo_sb[:, :, :], Wo.rearrange("(c p) n -> p c n", p=P)).then_inc(S["ld_wo"], 16)
            for dst, src in ((gates[:, 0:1], g_xattn), (gates[:, 1:2], g_ffn), (bo_sb[:, :], bo), (bs2_sb[:, :], bs2),
                             (br_sb[:, :], br)):
                sp.dma_start(dst, src.partition_broadcast(P)).then_inc(S["ld_small"], 16)
            sp.dma_start(wr_sb[:, :], Wr).then_inc(S["ld_wr"], 16)
            sp.dma_start(b1_raw, be1).then_inc(S["ld_be"], 16)
            sp.dma_start(b2_raw[:, :], be2).then_inc(S["ld_be"], 16)
            with nc.allow_non_contiguous_dma(reason="512 biases, one per partition"):
                sp.dma_start(bs1_sb[:, :], bs1.rearrange("(c p) -> p c", p=P)).then_inc(S["ld_ws"], 16)
            sp.dma_start(ws1_sb[:, :], Ws1).then_inc(S["ld_ws"], 16)
            sp.dma_start(ws2_sb[:, :, :], Ws2.rearrange("(c p) n -> p c n", p=P)).then_inc(S["ld_ws"], 16)
            sp.dma_start(we1_sb[:, :, :], We1.rearrange("e d n -> d e n")).then_inc(S["ld_we"], 16)
            sp.dma_start(we2_sb[:, :, :, :], We2.rearrange("e (c p) n -> p e c n", p=P)).then_inc(S["ld_we"], 16)
            sp.wait_ge(S["bias_zero"], 2)
            sp.wait_ge(S["bias_parts"], 3)
            sp.dma_start(bias_dram, b_parts[:, :, :]).then_inc(S["bias_out"], 16)
            sp.wait_ge(S["bias_out"], 16)
            by_part = bias_dram.rearrange("e t n -> t e n")
            sp.dma_start(b1_3[0:3, :, :], by_part[:, :, 0:HE]).then_inc(S["ld_b3"], 16)
            sp.dma_start(b2_3[0:3, :, :], by_part[:, :, HE:HE + D]).then_inc(S["ld_b3"], 16)

            sp.wait_ge(S["pad_ready"], 1)
            sp.wait_ge(S["consts"], 1)
            with sp.Fori(0, E) as e:
                r = sp.value_load(pad_i[0:1, bass.ds(e, 1)], min_val=0, max_val=E * CAP - P)
                sp.dma_start(slots[bass.ds(r, P), :], pad_row[:, :]).then_inc(S["pads_stored"], 16)
            sp.dma_start(slots[E * CAP:E * CAP + P, :], pad_row[:, :]).then_inc(S["pads_stored"], 16)
            sp.wait_ge(S["pads_stored"], 16 * (E + 1))
            for par in range(2):
                sp.wait_ge(scat[par], 16 * 4 * (B // 2))
            sp.wait_ge(S["table_done"], 2)

            def load(k, u):
                since(sp, k, 4, S["tokT_pe"], k - 3)
                since(sp, k, 4, S["meta_done"], k - 3)
                r = sp.value_load(row_i[0:1, bass.ds(k, 1)], min_val=0, max_val=E * CAP)
                sp.dma_start(tok[:, u, :], slots[bass.ds(r, P), :]).then_inc(tile_in[u], 16)

            for k in range(4):
                load(k, k)
            with sp.Fori(1, TILES // 4) as turn:
                for u in range(4):
                    load(turn * 4 + u, u)
            for k in range(TILES - 3, TILES):
                load(k, k % 4)

            for u in range(4):
                sp.wait_ge(tile_out[u], 16 * ((TILES - u + 3) // 4))
            cv = chosen.rearrange("(b p j k) d -> p b (j k d)", b=B, j=J, k=2)
            for n in range(4):
                w = B // 4
                sp.dma_start(ych[:, n * w:(n + 1) * w, :, :, :].rearrange("p b j k d -> p b (j k d)"),
                             cv[:, n * w:(n + 1) * w, :]).then_inc(ych_in[n], 16)
            ov = out.rearrange("b (p j) d -> p b j d", j=J)
            for n in range(4):
                w = B // 4
                sp.wait_ge(S["fin_done"], n + 1)
                sp.dma_start(ov[:, n * w:(n + 1) * w, :, :], fin[:, n * w:(n + 1) * w, :, :]).then_inc(S["stored"], 16)
            sp.wait_ge(S["stored"], 64)

        @block.gpsimd
        def _(pool):
            g = nc.gpsimd
            g.memset(ident[:, :], 0.0)
            g.memset(before[:, :], 1.0)
            g.memset(pad_row[:, :], 0.0)
            g.memset(one_row[:, :], 0.0)
            g.memset(three_rows[:, :], 0.0)
            g.memset(ones_b[:, :], 1.0)
            g.memset(eps_c[:, :], EPS)
            g.memset(x_sb[:, B:B + 2, :, :], 0.0)
            g.memset(seen[:, 0, :], 0.0)
            g.memset(tri_e[:, :, :], 1.0)
            g.iota(iota_e[:, :], [[1, E]], base=0, channel_multiplier=0, allow_small_or_imprecise_dtypes=True)
            g.iota(base_e[:, :], [[CAP, E]], base=0, channel_multiplier=0, allow_small_or_imprecise_dtypes=True)
            g.iota(tile_no[:, :], [[1, TILES]], base=0, channel_multiplier=0, allow_small_or_imprecise_dtypes=True)
            g.iota(dest_i[:, :, :, :], [[2 * T, B], [2, J], [1, 2]], base=0, channel_multiplier=2 * J
                   ).then_inc(S["chain"], 1)
            pool.wait_ge(S["chain"], 1)
            g.affine_select(out=ident[:, :], in_=ident[:, :], compare_op=ALU.not_equal, fill=1.0, base=0,
                            pattern=[[-1, P]], channel_multiplier=1)
            g.affine_select(out=before[:, :], in_=before[:, :], compare_op=ALU.is_gt, fill=0.0, base=0,
                            pattern=[[1, P]], channel_multiplier=-1)
            g.affine_select(out=tri_e[:, :, :], in_=tri_e[:, :, :], compare_op=ALU.is_ge, fill=0.0, base=0,
                            pattern=[[1, E], [-1, E]], channel_multiplier=0)
            g.memset(one_row[0:1, :], 1.0)
            g.memset(three_rows[0:3, :], 1.0)
            g.iota(pad_row[:, D + 1:D + 2].bitcast(I32), [[0, 1]], base=NOWHERE, channel_multiplier=0
                   ).then_inc(S["consts"], 1)
            g.memset(mask_add[:, :, :], 0.0).then_inc(S["mask_zero"], 1)
            g.memset(b1_3[:, :, :], 0.0).then_inc(S["bias_zero"], 1)
            g.memset(b2_3[:, :, :], 0.0).then_inc(S["bias_zero"], 1)
            pool.wait_ge(S["tg_done"], 1)
            pool.wait_ge(S["ld_small"], 80)
            pool.wait_ge(S["ld_x"], 16)
            g.tensor_scalar(bo_sb[:, :], bo_sb[:, :], tg[:, 0:1], None, ALU.mult).then_inc(S["xb_half"], 1)
            g.tensor_scalar(bs2_sb[:, :], bs2_sb[:, :], tg[:, 1:2], None, ALU.mult).then_inc(S["bs2t_done"], 1)
            pool.wait_ge(S["xb_half"], 1)
            for b in range(B):
                g.tensor_tensor(xb[:, b, :, :], x_sb[:, b, :, :], bo_sb[:, :].unsqueeze(1).to_broadcast([P, J, D]),
                                ALU.add).then_inc(S["xb_done"], 1)
            pool.wait_ge(S["bs2t_done"], 1)

            def step(s, par):
                if on(s, 0):
                    for j in range(J):
                        pool.wait_ge(S["srec_done"], s * J + (j + 1))
                        since(pool, s, 1, S["prT_pe"], s * J + (j - 1))
                        g.tensor_tensor(pr[:, j, :].rearrange("p (h k) -> p h k", h=HEADS),
                                        ex[:, j, :].rearrange("p (h k) -> p h k", h=HEADS),
                                        srec[:, par, j, :].unsqueeze(2).to_broadcast([P, HEADS, KEYS]),
                                        ALU.mult).then_inc(S["norm_done"], 1)
                if on(s, 1):
                    b = s - 1
                    q = 1 - par
                    pool.wait_ge(S["x1_done"], s)
                    g.tensor_tensor(pick(res, b), x1[:, q, :, :], bs2_sb[:, :].unsqueeze(1).to_broadcast([P, J, D]),
                                    ALU.add).then_inc(S["res0_done"], 1)
                    if not isinstance(s, int) or s >= 3:
                        apart(pool, (scat[q], (s - (1 + q)) * (16 * J)))
                    g.tensor_copy(payload[:, q, :, :, D + 1:D + 2].rearrange("p j k o -> p j (k o)").bitcast(I32),
                                  pick(dest_i, b)).then_inc(S["pay_meta"], 1)
                if on(s, 2):
                    b = s - 2
                    apart(pool, (S["slot_done"], s - 1), (S["pay_x"], (s - 1) * J), (S["gr_done"], (s - 1) * 2),
                          (S["pay_meta"], s - 1))
                    for j in range(J):
                        for k in range(2):
                            g.indirect_dma_start(
                                out=slots[:, :],
                                out_offset=bass.IndirectOffsetOnAxis(ap=slot_i[:, par, j, k:k + 1], axis=0),
                                in_=payload[:, par, j, k, :], in_offset=None).then_inc(scat[par], 16)

            steps(pool, step)

            def tile(i, u):
                if on(i, 0, TILES):
                    free = [] if isinstance(i, int) and i < 4 else [(tile_out[u], (i - u) * 4)]
                    apart(pool, (tile_in[u], (i - u) * 4 + 16), *free)
                    g.tensor_copy(meta[:, u, :].bitcast(I32), tok[:, u, D:D + 2].bitcast(I32)
                                  ).then_inc(S["meta_done"], 1)
                if on(i, 2, TILES):
                    v = (u - 2) % 4
                    apart(pool, (S["yt_done"], i - 1), (S["meta_done"], i - 1))
                    g.indirect_dma_start(
                        out=chosen[:, :],
                        out_offset=bass.IndirectOffsetOnAxis(ap=meta[:, v, 1:2].bitcast(U32), axis=0),
                        in_=yt[:, v, :], in_offset=None, bounds_check=2 * TOKENS - 1, oob_is_err=False
                    ).then_inc(tile_out[v], 16)

            tile_steps(pool, tile)

        @block.scalar
        def _(act):
            a = nc.scalar
            act.wait_ge(S["ld_small"], 80)
            a.activation(tg[:, :], gates[:, :], ACT.Tanh).then_inc(S["tg_done"], 1)
            act.wait_ge(S["mv1_done"], NT + 1)
            act.wait_ge(S["consts"], 1)
            a.activation(sd1[:, :, :], mv1[:, :, :, 1], ACT.Sqrt, bias=eps_c[:, 0:1]).then_inc(S["sd1_done"], 1)
            act.wait_ge(S["setup_pe"], 2)
            a.activation(wkT, bank[1][:, 0:4 * C].rearrange("p (c n) -> p c n", c=4), ACT.Copy
                         ).then_inc(S["setup_act"], 1)
            act.wait_ge(S["setup_pe"], 4)
            a.activation(wvT, bank[3][:, 0:4 * C].rearrange("p (c n) -> p c n", c=4), ACT.Copy
                         ).then_inc(S["setup_act"], 1)
            act.wait_ge(S["setup_pe"], 6)
            a.activation(a_sb[:, 1, :, :], bank[5][0:C, :].rearrange("p (c n) -> p c n", c=4), ACT.Copy
                         ).then_inc(S["setup_act"], 1)
            act.wait_ge(S["setup_pe"], 8)
            a.activation(bvo_sb[:, 1, :, :], bank[7][0:C, :].rearrange("p (c n) -> p c n", c=4), ACT.Copy
                         ).then_inc(S["setup_act"], 1)
            for h in range(1, HEADS, 2):
                act.wait_ge(S["fold_pe"], h + 1)
                a.activation(m_sb[:, :, h, :], bank[h % 4][:, :].rearrange("p (b k) -> p b k", b=B), ACT.Copy
                             ).then_inc(S["fold_evac"], 1)
            for n in range(1, 8, 2):
                act.wait_ge(S["fold_pe"], HEADS + n + 1)
                for half in range(2):
                    ins = a.activation(vw_sb[64:128, n // 2 * 2 + half, :, :],
                                       bank[4 + n % 4][64 * half:64 * half + 64, :].rearrange("p (c n) -> p c n", c=4),
                                       ACT.Copy)
                ins.then_inc(S["fold_evac"], 1)

            def normalise(b, par):
                since(act, b, 2, S["xnT_pe"], b - 1)
                for j in range(J):
                    a.activation(xn[:, par, j, :], pick(x_sb, b)[:, j, :], ACT.Identity,
                                 bias=pick(nb1, b)[:, j:j + 1], scale=pick(rs1, b)[:, j:j + 1]
                                 ).then_inc(S["xn_done"], 1)

            def keep_xnT(b, par):
                act.wait_ge(S["xnT_pe"], b + 1)
                since(act, b, 2, S["scores_pe"], (b - 1) * J)
                a.activation(xnT[:, par, :], bank[4][:, 0:J * P], ACT.Copy).then_inc(S["xnT_done"], 1)

            def exponent(s, j):
                act.wait_ge(S["shifted_done"], s * J + (j + 1))
                since(act, s, 1, S["norm_done"], s * J + (j - 1))
                a.activation(ex[:, j, :], shifted[:, j, :], ACT.Exp, scale=DH ** -0.5).then_inc(S["exp_done"], 1)

            def keep_prT(s, j):
                act.wait_ge(S["prT_pe"], s * J + (j + 1))
                since(act, s, 1, S["pv_pe"], s * J + (j - 1))
                a.activation(prT[:, j, :, :], bank[2 + j][:, :].rearrange("p (c n) -> p c n", c=4), ACT.Copy
                             ).then_inc(S["prT_done"], 1)

            act.wait_ge(S["rs1_done"], 1)
            normalise(0, 0)
            keep_xnT(0, 0)
            normalise(1, 1)

            def step(s, par):
                if on(s, 2):
                    act.wait_ge(S["x2T_pe"], s - 1)
                    a.activation(x2T_now[:, par, :], bank[5][:, 0:J * P], ACT.Copy).then_inc(S["x2T_done"], 1)
                if on(s, 0):
                    keep_xnT(s + 1, 1 - par)
                    exponent(s, 0)
                    exponent(s, 1)
                if on(s, 2):
                    a.activation(pick(x2T, s - 2), bank[5][:, 0:J * P], ACT.Copy).then_inc(S["x2T_kept"], 1)
                    act.wait_ge(S["gd_done"], s - 1)
                    a.activation(ge[:, :], gd[:, :], ACT.Exp, scale=1.0 / TAU).then_inc(S["ge_done"], 1)
                if on(s, 0):
                    normalise(s + 2, par)
                    keep_prT(s, 0)
                if on(s, 1):
                    q = 1 - par
                    act.wait_ge(S["mv2_done"], s * J)
                    a.activation(ln2[:, :], mv2[:, :, 1], ACT.Ln, bias=eps_c[:, 0:1]).then_inc(S["ln2_done"], 1)
                    act.wait_ge(S["ln2_done"], s)
                    a.activation(y2[:, :], ln2[:, :], ACT.Exp, scale=-0.5).then_inc(S["y2_done"], 1)
                if on(s, 0):
                    keep_prT(s, 1)
                if on(s, 1):
                    act.wait_ge(S["rs2_done"], s)
                    since(act, s, 3, scat[q], (s - (1 + q)) * (16 * J))
                    for j in range(J):
                        a.activation(payload[:, q, j, :, 0:D], x1[:, q, j, :].unsqueeze(1).to_broadcast([P, 2, D]),
                                     ACT.Identity, bias=nb2[:, j:j + 1], scale=ln2r[:, j:j + 1]
                                     ).then_inc(S["pay_x"], 1)

            a.add_instruction(mybir.InstLoadActFuncSet(name=nc.get_next_instruction_name(), act_func_set_id=6,
                                                       ins=[], outs=[]))
            steps(act, step)

            for c in range(4):
                for m in range(SC):
                    n = SC * c + m
                    act.wait_ge(S["up_pe"], n + 1)
                    if n >= 2:
                        act.wait_ge(S["hidS_done"], n - 1)
                    a.activation(gel[:, m, :], bank[m][:, :], ACT.Gelu, bias=bs1_sb[:, SC + m:SC + m + 1]
                                 ).then_inc(S["gel_done"], 1)
            U0 = 4 * SC

            def keep_tokT(k, par):
                act.wait_ge(S["tokT_pe"], k + 1)
                act.wait_ge(S["up_pe"], k + (U0 - 1))
                a.activation(tokT[:, par, :], bank[7][:, 0:P], ACT.Copy).then_inc(S["tokT_done"], 1)

            def tile(i, u):
                par = u % 2
                if on(i, -1, TILES):
                    keep_tokT(i + 1, 1 - par)
                if on(i, 0, TILES):
                    act.wait_ge(S["up_pe"], i + (U0 + 1))
                    if isinstance(i, int) and i < 2:
                        act.wait_ge(S["hidS_done"], U0)
                    else:
                        act.wait_ge(S["hid_done"], i - 1)
                    a.activation(gel[:, par, 0:HR], bank[par][:, 0:HR], ACT.Gelu).then_inc(S["gel_done"], 1)
                if on(i, 2, TILES):
                    v = (u - 2) % 4
                    act.wait_ge(S["y_pe"], i - 1)
                    act.wait_ge(S["meta_done"], i - 1)
                    since(act, i, 6, tile_out[v], (i - (2 + v)) * 4)
                    a.activation(yt[:, v, :], bank[4][:, 0:D], ACT.Copy, scale=meta[:, v, 0:1]
                                 ).then_inc(S["yt_done"], 1)

            keep_tokT(0, 0)
            tile_steps(act, tile)

        @block.vector
        def _(dve):
            v = nc.vector
            v.memset(mv1[:, B:B + 2, :, :], 0.0).then_inc(S["mv1_done"], 1)
            dve.wait_ge(S["ld_x"], 16)
            for t in range(NT):
                v.bn_stats(st1[:, t, :], x_sb[:, t // J, t % J, :]).then_inc(S["st1_done"], 1)
            dve.wait_ge(S["st1_done"], NT)
            for t in range(NT):
                v.bn_aggr(mv1[:, t // J, t % J, :], st1[:, t, :]).then_inc(S["mv1_done"], 1)
            dve.wait_ge(S["setup_pe"], 1)
            v.tensor_copy(wqT, bank[0][:, :].rearrange("p (c n) -> p c n", c=4)).then_inc(S["setup_dve"], 1)
            dve.wait_ge(S["setup_pe"], 3)
            v.tensor_copy(ctxT, bank[2][0:C, :]).then_inc(S["setup_dve"], 1)
            dve.wait_ge(S["sd1_done"], 1)
            v.reciprocal(rs1[:, :, :], sd1[:, :, :]).then_inc(S["chain_rs1"], 1)
            dve.wait_ge(S["chain_rs1"], 1)
            v.scalar_tensor_tensor(out=nb1[:, :, :], in0=mv1[:, :, :, 0], scalar=-1.0, in1=rs1[:, :, :], op0=ALU.mult,
                                   op1=ALU.mult).then_inc(S["rs1_done"], 1)

            dve.wait_ge(S["setup_pe"], 5)
            v.tensor_copy(a_sb[:, 0, :, :], bank[4][0:C, :].rearrange("p (c n) -> p c n", c=4)
                          ).then_inc(S["setup_dve"], 1)
            dve.wait_ge(S["setup_pe"], 7)
            v.tensor_copy(bvo_sb[:, 0, :, :], bank[6][0:C, :].rearrange("p (c n) -> p c n", c=4)
                          ).then_inc(S["setup_dve"], 1)
            dve.wait_ge(S["ld_mask"], 16)
            dve.wait_ge(S["mask_zero"], 1)
            v.tensor_scalar(mask_add[0:1, :, :], mask_sb[:, :, :], 0.0, MASKED, ALU.is_equal, ALU.mult).then_inc(S["mask_done"], 1)
            for h in range(0, HEADS, 2):
                dve.wait_ge(S["fold_pe"], h + 1)
                v.tensor_copy(m_sb[:, :, h, :], bank[h % 4][:, :].rearrange("p (b k) -> p b k", b=B)
                              ).then_inc(S["fold_evac_dve"], 1)
            for n in range(0, 8, 2):
                dve.wait_ge(S["fold_pe"], HEADS + n + 1)
                for half in range(2):
                    ins = v.tensor_copy(vw_sb[0:64, n // 2 * 2 + half, :, :],
                                        bank[4 + n % 4][64 * half:64 * half + 64, :].rearrange("p (c n) -> p c n", c=4))
                ins.then_inc(S["fold_evac_dve"], 1)
            dve.wait_ge(S["ld_be"], 32)
            for dst, lo in ((b1_raw, 0), (b2_raw[:, :], HE)):
                w = HE if lo == 0 else D
                v.tensor_copy(b_parts[:, 0, lo:lo + w], dst).then_inc(S["bias_rest"], 1)
            dve.wait_ge(S["bias_rest"], 2)
            for dst, lo in ((b1_raw, 0), (b2_raw[:, :], HE)):
                w = HE if lo == 0 else D
                v.tensor_tensor(b_rest[:, 0, lo:lo + w], dst, b_parts[:, 0, lo:lo + w], ALU.subtract
                                ).then_inc(S["bias_rest"], 1)
            dve.wait_ge(S["bias_rest"], 4)
            v.tensor_copy(b_parts[:, 1, :], b_rest[:, 0, :]).then_inc(S["bias_parts"], 1)
            dve.wait_ge(S["bias_parts"], 1)
            v.tensor_tensor(b_rest[:, 1, :], b_rest[:, 0, :], b_parts[:, 1, :], ALU.subtract).then_inc(S["bias_parts"], 1)
            dve.wait_ge(S["bias_parts"], 2)
            v.tensor_copy(b_parts[:, 2, :], b_rest[:, 1, :]).then_inc(S["bias_parts"], 1)

            def step(s, par):
                now, one, two = on(s, 0), on(s, 1), on(s, 2)
                n = s - 1
                q = 1 - par
                if now:
                    sc = [bank[j][:, :].rearrange("p (h k) -> p h k", h=HEADS) for j in range(J)]
                    for j in range(J):
                        dve.wait_ge(S["scores_pe"], s * J + (j + 1))
                        v.tensor_reduce(smax[:, par, j, :], sc[j], AX.X, ALU.max).then_inc(S["smax_done"], 1)
                    for j in range(J):
                        dve.wait_ge(S["smax_done"], s * J + (j + 1))
                        since(dve, s, 1, S["exp_done"], s * J + (j - 1))
                        v.tensor_tensor(shifted[:, j, :].rearrange("p (h k) -> p h k", h=HEADS), sc[j],
                                        smax[:, par, j, :].unsqueeze(2).to_broadcast([P, HEADS, KEYS]), ALU.subtract
                                        ).then_inc(S["shifted_done"], 1)

                def sum_exp(j):
                    dve.wait_ge(S["exp_done"], s * J + (j + 1))
                    v.tensor_reduce(ssum[:, par, j, :], ex[:, j, :].rearrange("p (h k) -> p h k", h=HEADS),
                                    AX.X, ALU.add).then_inc(S["ssum_done"], 1)

                def invert_sum(j):
                    dve.wait_ge(S["ssum_done"], s * J + (j + 1))
                    v.reciprocal(srec[:, par, j, :], ssum[:, par, j, :]).then_inc(S["srec_done"], 1)

                if two:
                    dve.wait_ge(S["logits_pe"], n)
                    v.tensor_tensor(lg[:, :, :], bank[7][:, 0:J * E].rearrange("p (j e) -> p j e", j=J),
                                    br_sb[:, :].unsqueeze(1).to_broadcast([P, J, E]), ALU.add).then_inc(S["lg_done"], 1)
                if now:
                    sum_exp(0)
                if two:
                    apart(dve, (S["lg_done"], n))
                    for j in range(J):
                        v.max(top[:, j, :], lg[:, j, :]).then_inc(S["top_done"], 1)
                if now:
                    invert_sum(0)
                if two:
                    apart(dve, (S["top_done"], n * J))
                    for j in range(J):
                        v.max_index(topi[:, j, :], top[:, j, :], lg[:, j, :]).then_inc(S["topi_done"], 1)
                    v.tensor_tensor(gd[:, :], top[:, :, 1], top[:, :, 0], ALU.subtract).then_inc(S["gd_done"], 1)
                if now:
                    sum_exp(1)
                if two:
                    dve.wait_ge(S["topi_done"], n * J)
                    v.tensor_copy(topf[:, :, :], topi[:, :, 0:2]).then_inc(S["topf_done"], 1)
                if now:
                    invert_sum(1)
                if two:
                    dve.wait_ge(S["topf_done"], n)
                    v.tensor_tensor(oh[:, :, :, :],
                                    iota_e[:, :].unsqueeze(1).unsqueeze(1).to_broadcast([P, J, 2, E]),
                                    topf[:, :, :].unsqueeze(3).to_broadcast([P, J, 2, E]), ALU.is_equal
                                    ).then_inc(S["oh_done"], 1)
                if one:
                    dve.wait_ge(S["pv_pe"], s * J)
                    since(dve, s, 3, S["res0_done"], s - 2)
                    if isinstance(s, int) and s == 1:
                        dve.wait_ge(S["xb_done"], B)
                    v.scalar_tensor_tensor(out=x1[:, q, :, :].rearrange("p j d -> p (j d)"), in0=bank[6][:, 0:J * D],
                                           scalar=tg[:, 0:1], in1=pick(xb, s - 1).rearrange("p j d -> p (j d)"),
                                           op0=ALU.mult, op1=ALU.add).then_inc(S["x1_done"], 1)
                if two:
                    dve.wait_ge(S["oh_done"], n)
                    v.tensor_tensor(hot[:, par, :, :], oh[:, :, 0, :], oh[:, :, 1, :], ALU.add).then_inc(S["hot_done"], 1)
                if one:
                    dve.wait_ge(S["x1_done"], s)
                    v.bn_stats(st2[:, 0, :], x1[:, q, 0, :]).then_inc(S["st2_done"], 1)
                if two:
                    dve.wait_ge(S["hot_done"], n)
                    v.tensor_tensor(seen_j[:, :], pick(seen, s - 2), hot[:, par, 0, :], ALU.add
                                    ).then_inc(S["seenj_done"], 1)
                if one:
                    v.bn_stats(st2[:, 1, :], x1[:, q, 1, :]).then_inc(S["st2_done"], 1)
                if two:
                    dve.wait_ge(S["seenj_done"], n)
                    v.tensor_tensor(pick(seen, s - 1), seen_j[:, :], hot[:, par, 1, :], ALU.add
                                    ).then_inc(S["seen_done"], 1)
                if one:
                    apart(dve, (S["st2_done"], s * J))
                    for j in range(J):
                        v.bn_aggr(mv2[:, j, :], st2[:, j, :]).then_inc(S["mv2_done"], 1)
                if two:
                    dve.wait_ge(S["ge_done"], n)
                    v.tensor_scalar(gz[:, :], ge[:, :], 1.0, None, ALU.add).then_inc(S["gz_done"], 1)
                    dve.wait_ge(S["pos_pe"], n)
                    v.tensor_tensor(pb[:, :, :], bank[7][:, 32:32 + J * E].rearrange("p (j e) -> p j e", j=J),
                                    base_e[:, :].unsqueeze(1).to_broadcast([P, J, E]), ALU.add).then_inc(S["pb_done"], 1)
                    dve.wait_ge(S["gz_done"], n)
                    v.reciprocal(gr[:, :], gz[:, :]).then_inc(S["gz2_done"], 1)
                    dve.wait_ge(S["pb_done"], n)
                    v.tensor_tensor(sl[:, :, :, :], oh[:, :, :, :], pb[:, :, :].unsqueeze(2).to_broadcast([P, J, 2, E]),
                                    ALU.mult).then_inc(S["sl_done"], 1)
                    dve.wait_ge(S["gz2_done"], n)
                    since(dve, s, 4, scat[par], (s - (2 + par)) * (16 * J))
                    v.tensor_scalar(payload[:, par, :, 0, D:D + 1].rearrange("p j o -> p (j o)"), gr[:, :], tg[:, 1:2],
                                    None, ALU.mult).then_inc(S["gr_done"], 1)
                    v.scalar_tensor_tensor(out=payload[:, par, :, 1, D:D + 1].rearrange("p j o -> p (j o)"),
                                           in0=gr[:, :], scalar=tg[:, 1:2], in1=ge[:, :], op0=ALU.mult,
                                           op1=ALU.mult).then_inc(S["gr_done"], 1)
                if one:
                    dve.wait_ge(S["y2_done"], s)
                    v.tensor_tensor(q2[:, :], y2[:, :], y2[:, :], ALU.mult).then_inc(S["q2a"], 1)
                if two:
                    dve.wait_ge(S["sl_done"], n)
                    v.tensor_reduce(slot_f[:, :, :], sl[:, :, :, :], AX.X, ALU.add).then_inc(S["slotf_done"], 1)
                if one:
                    dve.wait_ge(S["q2a"], s)
                    v.scalar_tensor_tensor(out=rs2[:, 0, :], in0=mv2[:, :, 1], scalar=EPS, in1=q2[:, :], op0=ALU.add,
                                           op1=ALU.mult).then_inc(S["q2b"], 1)
                if two:
                    dve.wait_ge(S["slotf_done"], n)
                    v.tensor_copy(slot_i[:, par, :, :], slot_f[:, :, :]).then_inc(S["slot_done"], 1)
                if one:
                    dve.wait_ge(S["q2b"], s)
                    v.tensor_scalar(rs2[:, 1, :], rs2[:, 0, :], -0.5, 1.5, ALU.mult, ALU.add).then_inc(S["q2c"], 1)
                    dve.wait_ge(S["q2c"], s)
                    since(dve, s, 2, S["pay_x"], (s - 1) * J)
                    v.tensor_tensor(ln2r[:, :], y2[:, :], rs2[:, 1, :], ALU.mult).then_inc(S["q2d"], 1)
                    dve.wait_ge(S["q2d"], s)
                    v.scalar_tensor_tensor(out=nb2[:, :], in0=mv2[:, :, 0], scalar=-1.0, in1=ln2r[:, :], op0=ALU.mult,
                                           op1=ALU.mult).then_inc(S["rs2_done"], 1)

            steps(dve, step)

            links = [1]

            def link(ins):
                links[0] += 1
                ins.then_inc(S["chain_dve"], 1)
                dve.wait_ge(S["chain_dve"], links[0] - 1)

            dve.wait_ge(S["cnt_pe"], 1)
            link(v.tensor_copy(cnt[:, :], bank[7][0:1, 64:64 + E]))
            v.tensor_tensor(pad_i[:, :], cnt[:, :], base_e[0:1, :], ALU.add).then_inc(S["pad_ready"], 1)
            link(v.tensor_scalar(til[:, :], cnt[:, :], float(P - 1), None, ALU.add))
            link(v.tensor_copy(cnt_i[:, 0, :], til[:, :]))
            link(v.tensor_scalar(cnt_i[:, 1, :], cnt_i[:, 0, :], 7, None, ALU.logical_shift_right))
            link(v.tensor_copy(til[:, :], cnt_i[:, 1, :]))
            link(v.tensor_tensor(tt[:, :, :], tri_e[:, :, :], til[:, :].unsqueeze(1).to_broadcast([1, E, E]), ALU.mult))
            link(v.tensor_reduce(cum[:, :], tt[:, :, :], AX.X, ALU.add))
            link(v.tensor_scalar(coef[:, :], til[:, :], -float(P), float(CAP), ALU.mult, ALU.add))
            link(v.tensor_tensor(ind[:, :, :], cum[:, :].unsqueeze(1).to_broadcast([1, TILES, E]),
                                 tile_no[:, :].unsqueeze(2).to_broadcast([1, TILES, E]), ALU.is_le))
            link(v.tensor_reduce(exp_f[:, :], ind[:, :, :], AX.X, ALU.add))
            v.tensor_scalar(exp_i[:, :], exp_f[:, :], float(E - 1), None, ALU.min).then_inc(S["table_done"], 1)
            link(v.tensor_tensor(indc[:, :, :], ind[:, :, :], coef[:, :].unsqueeze(1).to_broadcast([1, TILES, E]),
                                 ALU.mult))
            link(v.tensor_reduce(row_s[:, :], indc[:, :, :], AX.X, ALU.add))
            link(v.scalar_tensor_tensor(out=row_f[:, :], in0=tile_no[:, :], scalar=float(P), in1=row_s[:, :],
                                        op0=ALU.mult, op1=ALU.add))
            v.tensor_scalar(row_i[:, :], row_f[:, :], float(E * CAP), None, ALU.min).then_inc(S["table_done"], 1)

            def shared_hidden(c):
                for m in range(SC):
                    n = SC * c + m
                    dve.wait_ge(S["gel_done"], n + 1)
                    if c >= 2:
                        dve.wait_ge(S["yS_pe"], c - 1)
                    v.scalar_tensor_tensor(out=hid_s[c % 2][:, m, :], in0=bank[2 + m][:, :], scalar=bs1_sb[:, m:m + 1],
                                           in1=gel[:, m, :], op0=ALU.add, op1=ALU.mult).then_inc(S["hidS_done"], 1)

            shared_hidden(0)
            for c in range(4):
                if c < 3:
                    shared_hidden(c + 1)
                dve.wait_ge(S["yS_pe"], c + 1)
                if c == 0:
                    dve.wait_ge(S["res0_done"], B)
                o = res[:, 2 * c:2 * c + 2, :, :].rearrange("p b j d -> p (b j d)")
                v.scalar_tensor_tensor(out=o, in0=bank[4][:, :], scalar=tg[:, 1:2], in1=o, op0=ALU.mult, op1=ALU.add
                                       ).then_inc(S["yS_done"], 1)
            U0 = 4 * SC

            def tile(i, u):
                par = u % 2
                if on(i, 1, TILES):
                    dve.wait_ge(S["hidT_pe"], i)
                    since(dve, i, 3, S["y_pe"], i - 2)
                    v.tensor_copy(hidT[:, 1 - par, :], bank[6 - par][:, 0:HR]).then_inc(S["hidT_done"], 1)
                if on(i, 0, TILES):
                    dve.wait_ge(S["gel_done"], i + (U0 + 1))
                    since(dve, i, 2, S["hidT_pe"], i - 1)
                    v.tensor_tensor(hid[:, par, :], bank[2 + par][:, 0:HR], gel[:, par, 0:HR], ALU.mult
                                    ).then_inc(S["hid_done"], 1)

            tile_steps(dve, tile)

            for n in range(4):
                w = B // 4
                r = slice(n * w, (n + 1) * w)
                dve.wait_ge(ych_in[n], 16)
                v.tensor_tensor(fin[:, r, :, :], ych[:, r, :, 0, :], ych[:, r, :, 1, :], ALU.add).then_inc(S["fin_a"], 1)
                dve.wait_ge(S["fin_a"], n + 1)
                v.tensor_tensor(fin[:, r, :, :], fin[:, r, :, :], res[:, r, :, :], ALU.add).then_inc(S["fin_done"], 1)

        @block.tensor
        def _(pe):
            t = nc.tensor
            pe.wait_ge(S["consts"], 1)
            pe.wait_ge(S["ld_wq"], 16)
            for c in range(4):
                ins = t.transpose(bank[0][:, c * P:(c + 1) * P], wq_sb[:, c, :], ident[:, :])
            ins.then_inc(S["setup_pe"], 1)
            pe.wait_ge(S["ld_wk"], 16)
            for c in range(4):
                ins = t.transpose(bank[1][:, c * C:(c + 1) * C], wk_sb[:, c, :], ident[0:C, 0:C])
            ins.then_inc(S["setup_pe"], 1)
            pe.wait_ge(S["ld_ctx"], 16)
            for c in range(4):
                ins = t.transpose(bank[2][0:C, c * P:(c + 1) * P], ctx_sb[:, c, :], ident[:, :])
            ins.then_inc(S["setup_pe"], 1)
            pe.wait_ge(S["ld_wv"], 16)
            for c in range(4):
                ins = t.transpose(bank[3][:, c * C:(c + 1) * C], wv_sb[:, c, :], ident[0:C, 0:C])
            ins.then_inc(S["setup_pe"], 1)
            pe.wait_ge(S["setup_dve"], 1)
            pe.wait_ge(S["setup_act"], 1)
            for q in range(2):
                for c in range(4):
                    ins = t.matmul(bank[4 + q][0:C, c * P:(c + 1) * P], wkT[64 * q:64 * q + 64, c, :],
                                   wqT[64 * q:64 * q + 64, c, :], start=True, stop=True)
                ins.then_inc(S["setup_pe"], 1)
            pe.wait_ge(S["ld_wo"], 16)
            pe.wait_ge(S["setup_act"], 2)
            for q in range(2):
                for c in range(4):
                    ins = t.matmul(bank[6 + q][0:C, c * P:(c + 1) * P], wvT[64 * q:64 * q + 64, c, :],
                                   wo_sb[64 * q:64 * q + 64, c, :], start=True, stop=True)
                ins.then_inc(S["setup_pe"], 1)
            pe.wait_ge(S["setup_dve"], 3)
            pe.wait_ge(S["setup_act"], 3)
            for h in range(HEADS):
                if h >= 4:
                    pe.wait_ge(S["fold_evac_dve"] if h % 2 == 0 else S["fold_evac"], (h - 4) // 2 + 1)
                t.matmul(bank[h % 4][:, :], a_sb[:, h % 2, h // 2, :], ctxT, start=True, stop=True
                         ).then_inc(S["fold_pe"], 1)
            pe.wait_ge(S["setup_dve"], 4)
            pe.wait_ge(S["setup_act"], 4)
            for n in range(8):
                if n >= 4:
                    pe.wait_ge(S["fold_evac_dve"] if n % 2 == 0 else S["fold_evac"], 4 + (n - 4) // 2 + 1)
                t.matmul(bank[4 + n % 4][:, :], ctxT[:, n // 2 * P:(n // 2 + 1) * P],
                         bvo_sb[:, n % 2, :, :].rearrange("p c n -> p (c n)"), start=True, stop=True
                         ).then_inc(S["fold_pe"], 1)
            pe.wait_ge(S["fold_evac_dve"], 8)
            pe.wait_ge(S["fold_evac"], 8)
            pe.wait_ge(S["mask_done"], 1)
            pe.wait_ge(S["ld_wr"], 16)

            def turn_xn(b, par):
                pe.wait_ge(S["xn_done"], b * J + J)
                for j in range(J):
                    ins = t.transpose(bank[4][:, j * P:(j + 1) * P], xn[:, par, j, :], ident[:, :])
                ins.then_inc(S["xnT_pe"], 1)

            def turn_pr(s, j):
                pe.wait_ge(S["norm_done"], (s - 1) * J + (j + 1))
                for c in range(4):
                    ins = t.transpose(bank[2 + j][:, c * P:(c + 1) * P], pr[:, j, c * P:(c + 1) * P], ident[:, :])
                ins.then_inc(S["prT_pe"], 1)

            def attend(s, j):
                if j == 0:
                    since(pe, s, 2, S["x1_done"], s - 1)
                pe.wait_ge(S["prT_done"], (s - 1) * J + (j + 1))
                for c in range(4):
                    ins = t.matmul(bank[6][:, j * D:(j + 1) * D], prT[:, j, c, :], pick(vw_sb, s - 1)[:, c, :],
                                   start=(c == 0), stop=(c == 3))
                ins.then_inc(S["pv_pe"], 1)

            def score(s, par, j):
                since(pe, s, 1, S["shifted_done"], s * J + (j - 1))
                t.matmul(bank[j][:, :], xnT[:, par, j * P:(j + 1) * P],
                         pick(m_sb, s).rearrange("p h k -> p (h k)"), start=True, stop=False)
                t.matmul(bank[j][:, :], one_row[:, :],
                         pick(mask_add, s).unsqueeze(1).to_broadcast([P, HEADS, KEYS]), start=False, stop=True
                         ).then_inc(S["scores_pe"], 1)

            def rank(s, par):
                n = s - 2
                sv = pick(seen, s - 3)
                pe.wait_ge(S["lg_done"], n)
                pe.wait_ge(S["hot_done"], n)
                t.matmul(bank[7][:, 32:32 + E], ones_b[:, :], sv, start=True, stop=False)
                t.matmul(bank[7][:, 32:32 + E], before[:, :], hot[:, 1 - par, 0, :], start=False, stop=True)
                t.matmul(bank[7][:, 32 + E:32 + 2 * E], ones_b[:, :], sv, start=True, stop=False)
                t.matmul(bank[7][:, 32 + E:32 + 2 * E], ones_b[:, :], hot[:, 1 - par, 0, :], start=False, stop=False)
                t.matmul(bank[7][:, 32 + E:32 + 2 * E], before[:, :], hot[:, 1 - par, 1, :], start=False, stop=True
                         ).then_inc(S["pos_pe"], 1)

            def step(s, par):
                if on(s, 0):
                    pe.wait_ge(S["xnT_done"], s + 1)
                    score(s, par, 0)
                    score(s, par, 1)
                if on(s, 1):
                    turn_pr(s, 0)
                if on(s, 3):
                    rank(s, par)
                if on(s, 1):
                    turn_pr(s, 1)
                if on(s, 1):
                    attend(s, 0)
                if on(s, 2):
                    n = s - 1
                    pe.wait_ge(S["pay_x"], n * J)
                    since(pe, s, 3, S["x2T_kept"], n - 1)
                    for j in range(J):
                        ins = t.transpose(bank[5][:, j * P:(j + 1) * P], payload[:, par, j, 0, 0:D], ident[:, :])
                    ins.then_inc(S["x2T_pe"], 1)
                if on(s, 0):
                    turn_xn(s + 1, 1 - par)
                if on(s, 1):
                    attend(s, 1)
                if on(s, 2):
                    pe.wait_ge(S["x2T_done"], n)
                    since(pe, s, 3, S["pb_done"], n - 1)
                    for j in range(J):
                        ins = t.matmul(bank[7][:, j * E:(j + 1) * E], x2T_now[:, par, j * P:(j + 1) * P], wr_sb[:, :],
                                       start=True, stop=True)
                    ins.then_inc(S["logits_pe"], 1)

            turn_xn(0, 0)
            steps(pe, step)
            rank(B + 2, 0)

            pe.wait_ge(S["seen_done"], B)
            pe.wait_ge(S["pb_done"], B)
            t.matmul(bank[7][:, 64:64 + E], ones_b[:, :], seen[:, B, :], start=True, stop=True).then_inc(S["cnt_pe"], 1)

            pe.wait_ge(S["ld_ws"], 48)
            pe.wait_ge(S["ld_b3"], 32)
            pe.wait_ge(S["x2T_kept"], B)
            pe.wait_ge(S["shifted_done"], NT)
            pe.wait_ge(S["prT_done"], NT)

            def shared_up(c):
                for m in range(SC):
                    n = SC * c + m
                    if n >= 2:
                        pe.wait_ge(S["hidS_done"], n - 1)
                    xt = x2T[:, 2 * c:2 * c + 2, :].rearrange("p b n -> p (b n)")
                    t.matmul(bank[m][:, :], ws1_sb[:, (SC + m) * P:(SC + m + 1) * P], xt, start=True, stop=True)
                    t.matmul(bank[2 + m][:, :], ws1_sb[:, m * P:(m + 1) * P], xt, start=True, stop=True
                             ).then_inc(S["up_pe"], 1)

            shared_up(0)
            for c in range(4):
                if c < 3:
                    shared_up(c + 1)
                pe.wait_ge(S["hidS_done"], SC * (c + 1))
                if c:
                    pe.wait_ge(S["yS_done"], c)
                for n in range(4):
                    for m in range(SC):
                        ins = t.matmul(bank[4][:, n * D:(n + 1) * D], hid_s[c % 2][:, m, n * P:(n + 1) * P], ws2_sb[:, m, :],
                                       start=(m == 0), stop=(m == SC - 1))
                ins.then_inc(S["yS_pe"], 1)

            U0 = 4 * SC
            pe.wait_ge(S["ld_we"], 32)
            pe.wait_ge(S["table_done"], 2)
            pe.wait_ge(S["yS_done"], 4)
            pe.wait_ge(S["x1_done"], B)
            pe.wait_ge(S["chain_dve"], 1)

            def turn_tokens(k, u):
                pe.wait_ge(tile_in[u], (k - u) * 4 + 16)
                since(pe, k, 1, S["tokT_done"], k)
                t.transpose(bank[7][:, 0:P], tok[:, u, 0:D], ident[:, :]).then_inc(S["tokT_pe"], 1)

            def expert_of(k):
                return nc.values_load(exp_i[0:1, bass.ds(k, 1)], engines=(mybir.EngineType.PE,), min_val=0,
                                      max_val=E - 1, skip_runtime_bounds_check_because="a count, cut at E - 1")

            def tile(i, u):
                par = u % 2
                if on(i, 0, TILES):
                    e_up = expert_of(i)
                if on(i, -1, TILES):
                    turn_tokens(i + 1, (u + 1) % 4)
                if on(i, 0, TILES):
                    w = pick(we1_sb, e_up)
                    bias = pick(b1_3, e_up)
                    pe.wait_ge(S["tokT_done"], i + 1)
                    if isinstance(i, int) and i < 2:
                        pe.wait_ge(S["hidS_done"], U0)
                    else:
                        pe.wait_ge(S["hid_done"], i - 1)
                    t.matmul(bank[par][:, 0:HR], tokT[:, par, :], w[:, HR:HE], start=True, stop=False)
                    t.matmul(bank[par][:, 0:HR], three_rows[:, :], bias[:, HR:HE], start=False, stop=True)
                    t.matmul(bank[2 + par][:, 0:HR], tokT[:, par, :], w[:, 0:HR], start=True, stop=False)
                if on(i, 2, TILES):
                    e_down = expert_of(i - 2)
                if on(i, 0, TILES):
                    t.matmul(bank[2 + par][:, 0:HR], three_rows[:, :], bias[:, 0:HR], start=False, stop=True
                             ).then_inc(S["up_pe"], 1)
                if on(i, 1, TILES):
                    pe.wait_ge(S["hid_done"], i)
                    since(pe, i, 3, S["hidT_done"], i - 2)
                    for c in range(RC):
                        ins = t.transpose(bank[6 - par][:, c * P:(c + 1) * P], hid[:, 1 - par, c * P:(c + 1) * P],
                                          ident[:, :])
                    ins.then_inc(S["hidT_pe"], 1)
                if on(i, 2, TILES):
                    w = pick(we2_sb, e_down)
                    pe.wait_ge(S["hidT_done"], i - 1)
                    since(pe, i, 3, S["yt_done"], i - 2)
                    for c in range(RC):
                        t.matmul(bank[4][:, 0:D], hidT[:, par, c * P:(c + 1) * P], w[:, c, :], start=(c == 0),
                                 stop=False)
                    t.matmul(bank[4][:, 0:D], three_rows[:, :], pick(b2_3, e_down), start=False, stop=True
                             ).then_inc(S["y_pe"], 1)

            turn_tokens(0, 0)
            tile_steps(pe, tile)


_INS = ["x", "ctx_768", "mask_BxS2_bk0", "g_xattn", "g_ffn", "L0_xattn_W_q", "L0_xattn_W_k", "L0_xattn_W_v",
        "L0_xattn_W_o", "L0_xattn_b_o", "L0_ffn_Ws1", "L0_ffn_bs1", "L0_ffn_Ws2", "L0_ffn_bs2", "L0_ffn_We1",
        "L0_ffn_be1", "L0_ffn_We2", "L0_ffn_be2", "L0_ffn_Wr", "L0_ffn_br"]


def kernel(**inputs):
    import numpy as np
    import concourse.bacc as bacc
    from concourse.bass_utils import run_bass_kernel_spmd

    nc = bacc.Bacc("TRN2", target_bir_lowering=False, num_devices=1)
    arrays, args = {}, []
    for name in _INS:
        a = np.ascontiguousarray(inputs[name])
        arrays[f"in_{name}"] = a
        args.append(nc.dram_tensor(f"in_{name}", a.shape, mybir.dt.from_np(a.dtype), kind="ExternalInput").ap())
    shape = inputs["x"].shape
    out = nc.dram_tensor("out_dram", shape, F32, kind="ExternalOutput").ap()
    flamingo_block(nc, *args, out)
    return run_bass_kernel_spmd(nc, [arrays], core_ids=[0]).results[0]["out_dram"]
```

```python
from contextlib import ExitStack

import concourse.bass as bass
from concourse import mybir

F32 = mybir.dt.float32
BF16 = mybir.dt.bfloat16
F32R = mybir.dt.float32r
I32 = mybir.dt.int32
U32 = mybir.dt.uint32
U8 = mybir.dt.uint8
ALU = mybir.AluOpType
ACT = mybir.ActivationFunctionType
AX = mybir.AxisListType

P = 128
HEADS = 8
DH = 64
TAU = 1.5
EPS = 1e-5
MASKED = -float(2 ** 120)
FIN_VECTOR, FIN_POOL = (0, 1, 3, 4, 6, 7), (2, 5)
FOLD_BANK = (6, 7, 2, 3, 5, 7, 5, 7)
NOWHERE = 1 << 20


def flamingo_block(nc, x, ctx, mask, g_xattn, g_ffn, Wq, Wk, Wv, Wo, bo,
                   Ws1, bs1, Ws2, bs2, We1, be1, We2, be2, Wr, br, out):
    B, T, D = x.shape
    KEYS, C = ctx.shape[1:]
    E, _, HE = We1.shape
    HS = Ws1.shape[1]
    HR, HSH = HE // 2, HS // 2
    RC = HR // P
    SC = HSH // P
    TOKENS = B * T
    J = T // P
    NT = B * J
    CAP = TOKENS + P
    ROW = D + 2
    TILES = (2 * TOKENS + E * (P - 1)) // P
    assert D == P and T % P == 0 and HEADS * DH == Wq.shape[1] and HEADS * KEYS == 512
    assert J == 2 and SC == 2 and TILES % 4 == 3 and B % 2 == 0

    slots = nc.dram_tensor("slots", [E * CAP + P, ROW], F32).ap()
    bias_dram = nc.dram_tensor("bias_dram", [E, 3, HE + D], BF16).ap()
    chosen = nc.dram_tensor("chosen", [2 * TOKENS, D], F32).ap()

    with ExitStack() as stack:
        def sb(name, shape, dt=F32):
            return stack.enter_context(nc.sbuf_tensor(name, shape, dt))

        def sem(name):
            return stack.enter_context(nc.semaphore(name))

        bank = [stack.enter_context(nc.psum_tensor(f"bank{i}", [P, 512], F32)) for i in range(8)]

        sizes = [(B + 2) * J * D, B * HEADS * KEYS, B * 4 * D]
        room = sb("room", [P, sum(sizes)])
        we1_hi = room[:, 0:E * HE].bitcast(F32R).rearrange("p (e n) -> p e n", e=E)
        x_sb = room[:, 0:sizes[0]].rearrange("p (b j d) -> p b j d", b=B + 2, j=J)
        ctx_sb = sb("ctx_sb", [P, B * KEYS // P, C])
        wq_sb = sb("wq_sb", [P, 4, P])
        wk_sb = sb("wk_sb", [C, 4, P])
        wv_sb = sb("wv_sb", [C, 4, P])
        wo_sb = sb("wo_sb", [P, 4, D])
        mask_sb = sb("mask_sb", [1, B, KEYS], U8)
        mask_add = sb("mask_add", [1, B, KEYS], BF16)
        bo_sb = sb("bo_sb", [P, D])
        bs2_sb = sb("bs2_sb", [P, D])
        br_sb = sb("br_sb", [P, E])
        bs1_sb = sb("bs1_sb", [P, 4])
        gates = sb("gates", [P, 2])
        tg = sb("tg", [P, 2])
        wr_sb = sb("wr_sb", [P, E])
        ws1_sb = sb("ws1_sb", [P, HS])
        ws2_sb = sb("ws2_sb", [P, SC, D])
        we1_sb = sb("we1_sb", [P, E, HE])
        we1_lo = we1_sb[:, :, :].bitcast(F32R)
        we2_sb = sb("we2_sb", [P, E, RC, D])
        b2_raw = sb("b2_raw", [E, D])
        b1_3 = sb("b1_3", [3, E, HE], BF16)
        b2_3 = sb("b2_3", [3, E, D], BF16)
        b_parts = sb("b_parts", [E, 3, HE + D], BF16)

        ident = sb("ident", [P, P])
        before = sb("before", [P, P], BF16)
        ones_b = sb("ones_b", [P, P], BF16)
        one_row = sb("one_row", [1, P], BF16)
        three_rows = sb("three_rows", [3, P], BF16)
        iota_e = sb("iota_e", [P, E])
        base_e = sb("base_e", [P, E])
        eps_c = sb("eps_c", [P, 1])
        pad_row = sb("pad_row", [P, ROW])
        dest_i = sb("dest_i", [P, B, J, 2], I32)

        m_sb = room[:, sizes[0]:sizes[0] + sizes[1]].rearrange("p (b h k) -> p b h k", b=B, h=HEADS)
        vw_sb = room[:, sizes[0] + sizes[1]:sum(sizes)].rearrange("p (b c d) -> p b c d", b=B, c=4)

        st1 = sb("st1", [P, NT, 6])
        mv1 = sb("mv1", [P, B + 2, J, 2])
        ln1 = sb("ln1", [P, B + 2, J])
        y1 = sb("y1", [P, B + 2, J])
        q1 = sb("q1", [P, 3, B + 2, J])
        rs1 = sb("rs1", [P, B + 2, J])
        nb1 = sb("nb1", [P, B + 2, J])
        xn = sb("xn", [P, 2, J, D])
        xb = sb("xb", [P, B, J, D])
        res = xb
        x1 = sb("x1", [P, 2, J, D])
        xnT = sb("xnT", [P, 2, J * P])
        x2T = sb("x2T", [P, B, J * P])
        x2T_now = sb("x2T_now", [P, 2, J * P])
        ln2r = sb("ln2r", [P, J])
        smax = sb("smax", [P, 2, J, HEADS])
        ssum = sb("ssum", [P, 2, J, HEADS])
        srec = sb("srec", [P, 2, J, HEADS])
        shifted = sb("shifted", [P, J, 512])
        ex = sb("ex", [P, J, 512])
        pr = sb("pr", [P, J, 512])
        prT = sb("prT", [P, J, 4, P])
        flat = [b[:, :, :].rearrange("p j n -> p (j n)") for b in (shifted, ex, pr)]
        flat.append(prT[:, :, :, :].rearrange("p j c n -> p (j c n)"))
        wqT = flat[0][:, 0:4 * P].rearrange("p (c n) -> p c n", c=4)
        wkT = flat[0][:, 4 * P:4 * (P + C)].rearrange("p (c n) -> p c n", c=4)
        a_sb = flat[1][0:C, :].rearrange("p (q c n) -> p q c n", q=2, c=4)
        wvT = flat[3][:, 0:4 * C].rearrange("p (c n) -> p c n", c=4)
        ctxT = x1[:, :, :, :].rearrange("p a j d -> p (a j d)")[0:C, 0:B * KEYS]
        st2 = sb("st2", [P, J, 6])
        mv2 = sb("mv2", [P, J, 2])
        ln2 = sb("ln2", [P, J])
        nb2 = sb("nb2", [P, J])
        y2 = sb("y2", [P, J])
        q2 = sb("q2", [P, J])
        rs2 = sb("rs2", [P, 2, J])
        payload = sb("payload", [P, 2, J, 2, ROW])
        bvo_sb = payload[:, :, :, :, :].rearrange("p a j k r -> p (a j k r)")[0:C, 0:8 * P].rearrange(
            "p (q c n) -> p q c n", q=2, c=4)
        lg = sb("lg", [P, J, E])
        top = sb("top", [P, J, 8])
        topi = sb("topi", [P, J, 8], U32)
        topf = sb("topf", [P, J, 2])
        gd = sb("gd", [P, J])
        ge = sb("ge", [P, J])
        gz = sb("gz", [P, J])
        gr = sb("gr", [P, J])
        oh = sb("oh", [P, J, 2, E])
        hot = sb("hot", [P, 2, J, E], BF16)
        seen = sb("seen", [P, B + 1, E], BF16)
        seen_j = sb("seen_j", [P, E], BF16)
        pb = sb("pb", [P, J, E])
        sl = sb("sl", [P, J, 2, E])
        slot_f = sb("slot_f", [P, J, 2])
        slot_i = sb("slot_i", [P, 2, J, 2], U32)

        cnt = sb("cnt", [1, E])
        pad_i = sb("pad_i", [1, E], I32)
        cnt_i = sb("cnt_i", [1, 2, E], I32)
        til = sb("til", [1, E])
        tri_e = sb("tri_e", [1, E, E])
        tt = sb("tt", [1, E, E])
        cum = sb("cum", [1, E])
        coef = sb("coef", [1, E])
        tile_no = sb("tile_no", [1, TILES])
        exp_f = sb("exp_f", [1, TILES])
        exp_i = sb("exp_i", [1, TILES], I32)
        row_s = sb("row_s", [1, TILES])
        row_f = sb("row_f", [1, TILES])
        row_i = sb("row_i", [1, TILES], I32)

        tok = sb("tok", [P, 4, ROW])
        tokT = sb("tokT", [P, 2, 2, P], F32R)
        hidT = sb("hidT", [P, 2, HR])
        b1_raw = hidT[0:E, :, :].rearrange("p a n -> p (a n)")
        work = sb("work", [P, 2 * (HE + D)])
        b_rest = work[0:E, :].rearrange("p (a n) -> p a n", a=2)
        gel = work[:, 0:1024].rearrange("p (a n) -> p a n", a=2)
        hid = work[:, 1024:1024 + 2 * HR].rearrange("p (a n) -> p a n", a=2)
        hid_s = (ex, prT[:, :, :, :].rearrange("p j c n -> p j (c n)"))
        ind = shifted[0:1, :, :].rearrange("p j n -> p (j n)")[:, 0:TILES * E].rearrange("p (t e) -> p t e", e=E)
        indc = pr[0:1, :, :].rearrange("p j n -> p (j n)")[:, 0:TILES * E].rearrange("p (t e) -> p t e", e=E)
        meta = sb("meta", [P, 4, 2])
        yt = sb("yt", [P, 4, D])
        ych = m_sb[:, :, :, :].rearrange("p b h (q k) -> p b (h q k)", q=1).rearrange(
            "p b (j k d) -> p b j k d", j=J, k=2)
        fin = vw_sb[:, 0:B // 2, :, :].rearrange("p b c d -> p (b c d)").rearrange("p (b j d) -> p b j d", b=B, j=J)

        names = """ld_x ld_ctx ld_wq ld_wk ld_wv ld_wo ld_mask ld_small ld_wr ld_ws ld_we ld_be ld_b3 bias_out ones_set
        consts mask_done bias_parts bias_rest setup_pe setup_act setup_dve fold_pe fold_evac
        fold_evac_dve st1_done mv1_done ln1_done y1_done newton1 rs1_done xn_done xb_half xb_done
        tg_done bs2t_done xnT_pe xnT_done scores_pe smax_done shifted_done exp_done ssum_done
        srec_done norm_done prT_pe prT_done pv_pe x1_done st2_done mv2_done ln2_done y2_done q2a q2b
        q2c q2d gz2_done rs2_done x2T_kept pay_x pay_meta res0_done x2T_pe x2T_done logits_pe
        lg_done top_done topi_done topf_done gd_done ge_done gz_done gr_done oh_done hot_done
        seenj_done seen_done pos_pe pb_done sl_done slotf_done slot_done cnt_pe chain chain_dve
        apart_dve apart_pool pad_ready table_done pads_stored we_hi we_lo_pool we_lo_dve tokT_hi
        up_pe gel_done hidS_done yS_pe yS_done tokT_pe tokT_done meta_done hid_done hidT_pe
        hidT_done y_pe yt_done fin_a fin_pool stored""".split()
        S = {n: sem(n) for n in names}
        scat = [sem(f"rows_scattered{i}") for i in range(2)]
        tile_in = [sem(f"tile_loaded{i}") for i in range(4)]
        tile_out = [sem(f"results_scattered{i}") for i in range(4)]
        fin_done = [sem(f"batch_finished{i}") for i in range(B)]
        ych_in = [sem(f"choices_loaded{i}") for i in range(B)]

        def steps(eng, body):
            for s in range(4):
                body(s, s % 2)
            with eng.Fori(2, B // 2) as pair:
                body(pair * 2, 0)
                body(pair * 2 + 1, 1)
            body(B, 0)
            body(B + 1, 1)

        def on(s, lag, count=B):
            return not isinstance(s, int) or 0 <= s - lag < count

        def tile_steps(eng, body):
            for i in range(6):
                body(i, i % 4)
            with eng.Fori(1, (TILES - 3) // 4) as turn:
                for n in range(4):
                    body(turn * 4 + (2 + n), (2 + n) % 4)
            for i in range(TILES - 1, TILES + 2):
                body(i, i % 4)

        def since(eng, s, first, semaphore, count):
            if not isinstance(s, int) or s >= first:
                eng.wait_ge(semaphore, count)

        def apart(eng, *waits):
            for semaphore, count in waits:
                eng.wait_ge(semaphore, count)
            eng.sem_inc(S["apart_dve" if eng is nc.vector else "apart_pool"], 1)

        def pick(t, b):
            if isinstance(b, int):
                return t[:, b]
            v = t[:, bass.ds(b, 1)]
            dims = ["c", "d", "e"][:len(v.shape) - 2]
            return v.rearrange(f"p a {' '.join(dims)} -> p (a {dims[0]}) {' '.join(dims[1:])}")

        block = stack.enter_context(nc.Block())

        @block.sync
        def _(sp):
            xv = x.rearrange("b (p j) d -> p b j d", j=J)
            sp.dma_start(wq_sb[:, :, :], Wq.rearrange("d (c n) -> d c n", c=4)).then_inc(S["ld_wq"], 16)
            sp.dma_start(wk_sb[:, :, :], Wk.rearrange("d (c n) -> d c n", c=4)).then_inc(S["ld_wk"], 16)
            sp.dma_start(ctx_sb[:, :, :], ctx.rearrange("b k c -> (b k) c").rearrange("(t p) c -> p t c", p=P)
                         ).then_inc(S["ld_ctx"], 16)
            sp.dma_start(x_sb[:, 0:B, :, :], xv).then_inc(S["ld_x"], 16)
            sp.dma_start(mask_sb[:, :, :], mask.unsqueeze(0)).then_inc(S["ld_mask"], 16)
            sp.dma_start(wv_sb[:, :, :], Wv.rearrange("d (c n) -> d c n", c=4)).then_inc(S["ld_wv"], 16)
            sp.dma_start(wo_sb[:, :, :], Wo.rearrange("(c p) n -> p c n", p=P)).then_inc(S["ld_wo"], 16)
            for dst, src in ((gates[:, 0:1], g_xattn), (gates[:, 1:2], g_ffn), (bo_sb[:, :], bo), (bs2_sb[:, :], bs2),
                             (br_sb[:, :], br)):
                sp.dma_start(dst, src.partition_broadcast(P)).then_inc(S["ld_small"], 16)
            sp.dma_start(wr_sb[:, :], Wr).then_inc(S["ld_wr"], 16)
            sp.dma_start(b1_raw, be1).then_inc(S["ld_be"], 16)
            sp.dma_start(b2_raw[:, :], be2).then_inc(S["ld_be"], 16)
            with nc.allow_non_contiguous_dma(reason="512 biases, one per partition"):
                sp.dma_start(bs1_sb[:, :], bs1.rearrange("(c p) -> p c", p=P)).then_inc(S["ld_ws"], 16)
            sp.dma_start(ws1_sb[:, :], Ws1).then_inc(S["ld_ws"], 16)
            sp.dma_start(ws2_sb[:, :, :], Ws2.rearrange("(c p) n -> p c n", p=P)).then_inc(S["ld_ws"], 16)
            sp.dma_start(we1_sb[:, :, :], We1.rearrange("e d n -> d e n")).then_inc(S["ld_we"], 16)
            sp.dma_start(we2_sb[:, :, :, :], We2.rearrange("e (c p) n -> p e c n", p=P)).then_inc(S["ld_we"], 16)
            sp.wait_ge(S["bias_parts"], 3)
            sp.dma_start(bias_dram, b_parts[:, :, :]).then_inc(S["bias_out"], 16)
            sp.wait_ge(S["bias_out"], 16)
            by_part = bias_dram.rearrange("e t n -> t e n")
            sp.dma_start(b1_3[0:3, :, :], by_part[:, :, 0:HE]).then_inc(S["ld_b3"], 16)
            sp.dma_start(b2_3[0:3, :, :], by_part[:, :, HE:HE + D]).then_inc(S["ld_b3"], 16)

            sp.dma_start(slots[E * CAP:E * CAP + P, :], pad_row[:, :]).then_inc(S["pads_stored"], 16)
            sp.wait_ge(S["pad_ready"], 1)
            sp.wait_ge(S["consts"], 1)
            with sp.Fori(0, E // 4) as quad:
                for n in range(4):
                    r = nc.values_load(pad_i[0:1, bass.ds(quad * 4 + n, 1)], engines=(mybir.EngineType.SP,), min_val=0,
                                       max_val=E * CAP - P, skip_runtime_bounds_check_because="a region has CAP rows")
                    sp.dma_start(slots[bass.ds(r, P), :], pad_row[:, :]).then_inc(S["pads_stored"], 16)
            sp.wait_ge(S["pads_stored"], 16 * (E + 1))
            for par in range(2):
                sp.wait_ge(scat[par], 16 * 4 * (B // 2))
            sp.wait_ge(S["table_done"], 2)

            def load(k, u):
                since(sp, k, 4, S["tokT_pe"], k - 3)
                since(sp, k, 4, S["meta_done"], k - 3)
                r = nc.values_load(row_i[0:1, bass.ds(k, 1)], engines=(mybir.EngineType.SP,), min_val=0,
                                   max_val=E * CAP, skip_runtime_bounds_check_because="cut at E * CAP")
                sp.dma_start(tok[:, u, :], slots[bass.ds(r, P), :]).then_inc(tile_in[u], 16)

            for k in range(4):
                load(k, k)
            with sp.Fori(1, TILES // 4) as turn:
                for u in range(4):
                    load(turn * 4 + u, u)
            for k in range(TILES - 3, TILES):
                load(k, k % 4)

            for u in range(4):
                sp.wait_ge(tile_out[u], 16 * ((TILES - u + 3) // 4))
            cv = chosen.rearrange("(b p j k) d -> p b (j k d)", b=B, j=J, k=2)
            for b in range(B):
                sp.dma_start(ych[:, b, :, :, :].rearrange("p j k d -> p (j k d)"), cv[:, b, :]).then_inc(ych_in[b], 16)
            ov = out.rearrange("b (p j) d -> p b j d", j=J)
            for b in range(B):
                sp.wait_ge(fin_done[b], 1)
                sp.dma_start(ov[:, b, :, :], fin[:, b, :, :]).then_inc(S["stored"], 16)
            sp.wait_ge(S["stored"], 16 * B)

        @block.gpsimd
        def _(pool):
            g = nc.gpsimd
            g.memset(ones_b[:, :], 1.0).then_inc(S["ones_set"], 1)
            g.memset(ident[:, :], 0.0)
            g.memset(before[:, :], 1.0)
            g.memset(pad_row[:, :], 0.0)
            g.memset(one_row[:, :], 1.0)
            g.memset(three_rows[:, :], 1.0)
            g.memset(eps_c[:, :], EPS)
            g.memset(x_sb[:, B:B + 2, :, :], 0.0)
            g.memset(seen[:, 0, :], 0.0)
            g.memset(tri_e[:, :, :], 1.0)
            g.iota(iota_e[:, :], [[1, E]], base=0, channel_multiplier=0, allow_small_or_imprecise_dtypes=True)
            g.iota(base_e[:, :], [[CAP, E]], base=0, channel_multiplier=0, allow_small_or_imprecise_dtypes=True)
            g.iota(tile_no[:, :], [[1, TILES]], base=0, channel_multiplier=0, allow_small_or_imprecise_dtypes=True)
            g.iota(dest_i[:, :, :, :], [[2 * T, B], [2, J], [1, 2]], base=0, channel_multiplier=2 * J
                   ).then_inc(S["chain"], 1)
            pool.wait_ge(S["chain"], 1)
            g.affine_select(out=ident[:, :], in_=ident[:, :], compare_op=ALU.not_equal, fill=1.0, base=0,
                            pattern=[[-1, P]], channel_multiplier=1)
            g.affine_select(out=before[:, :], in_=before[:, :], compare_op=ALU.is_gt, fill=0.0, base=0,
                            pattern=[[1, P]], channel_multiplier=-1)
            g.affine_select(out=tri_e[:, :, :], in_=tri_e[:, :, :], compare_op=ALU.is_ge, fill=0.0, base=0,
                            pattern=[[1, E], [-1, E]], channel_multiplier=0)
            g.iota(pad_row[:, D + 1:D + 2].bitcast(I32), [[0, 1]], base=NOWHERE, channel_multiplier=0
                   ).then_inc(S["consts"], 1)
            pool.wait_ge(S["tg_done"], 1)
            pool.wait_ge(S["ld_small"], 80)
            pool.wait_ge(S["ld_x"], 16)
            g.tensor_scalar(bo_sb[:, :], bo_sb[:, :], tg[:, 0:1], None, ALU.mult).then_inc(S["xb_half"], 1)
            g.tensor_scalar(bs2_sb[:, :], bs2_sb[:, :], tg[:, 1:2], None, ALU.mult).then_inc(S["bs2t_done"], 1)
            pool.wait_ge(S["xb_half"], 1)
            for b in range(B):
                g.tensor_tensor(xb[:, b, :, :], x_sb[:, b, :, :], bo_sb[:, :].unsqueeze(1).to_broadcast([P, J, D]),
                                ALU.add).then_inc(S["xb_done"], 1)
            pool.wait_ge(S["bs2t_done"], 1)

            def step(s, par):
                if on(s, 0):
                    for j in range(J):
                        pool.wait_ge(S["srec_done"], s * J + (j + 1))
                        since(pool, s, 1, S["prT_pe"], s * J + (j - 1))
                        g.tensor_tensor(pr[:, j, :].rearrange("p (h k) -> p h k", h=HEADS),
                                        ex[:, j, :].rearrange("p (h k) -> p h k", h=HEADS),
                                        srec[:, par, j, :].unsqueeze(2).to_broadcast([P, HEADS, KEYS]),
                                        ALU.mult).then_inc(S["norm_done"], 1)
                if on(s, 1):
                    b = s - 1
                    q = 1 - par
                    pool.wait_ge(S["x1_done"], s)
                    g.tensor_tensor(pick(res, b), x1[:, q, :, :], bs2_sb[:, :].unsqueeze(1).to_broadcast([P, J, D]),
                                    ALU.add).then_inc(S["res0_done"], 1)
                    if not isinstance(s, int) or s >= 3:
                        apart(pool, (scat[q], (s - (1 + q)) * (16 * J)))
                    g.tensor_copy(payload[:, q, :, :, D + 1:D + 2].rearrange("p j k o -> p j (k o)").bitcast(I32),
                                  pick(dest_i, b)).then_inc(S["pay_meta"], 1)
                if on(s, 2):
                    b = s - 2
                    apart(pool, (S["slot_done"], s - 1), (S["pay_x"], (s - 1) * J), (S["gr_done"], (s - 1) * 2),
                          (S["pay_meta"], s - 1))
                    for j in range(J):
                        for k in range(2):
                            g.indirect_dma_start(
                                out=slots[:, :],
                                out_offset=bass.IndirectOffsetOnAxis(ap=slot_i[:, par, j, k:k + 1], axis=0),
                                in_=payload[:, par, j, k, :], in_offset=None).then_inc(scat[par], 16)

            steps(pool, step)
            for e in range(8):
                pool.wait_ge(S["we_hi"], e + 1)
                g.tensor_tensor(we1_lo[:, e, :], we1_sb[:, e, :], we1_hi[:, e, :].bitcast(F32), ALU.subtract
                                ).then_inc(S["we_lo_pool"], 1)

            def tile(i, u):
                if on(i, 0, TILES):
                    free = [] if isinstance(i, int) and i < 4 else [(tile_out[u], (i - u) * 4)]
                    apart(pool, (tile_in[u], (i - u) * 4 + 16), *free)
                    g.tensor_copy(meta[:, u, :].bitcast(I32), tok[:, u, D:D + 2].bitcast(I32)
                                  ).then_inc(S["meta_done"], 1)
                if on(i, 2, TILES):
                    v = (u - 2) % 4
                    apart(pool, (S["yt_done"], i - 1), (S["meta_done"], i - 1))
                    g.indirect_dma_start(
                        out=chosen[:, :],
                        out_offset=bass.IndirectOffsetOnAxis(ap=meta[:, v, 1:2].bitcast(U32), axis=0),
                        in_=yt[:, v, :], in_offset=None, bounds_check=2 * TOKENS - 1, oob_is_err=False
                    ).then_inc(tile_out[v], 16)

            tile_steps(pool, tile)

            for b in FIN_POOL:
                pool.wait_ge(ych_in[b], 16)
                g.tensor_tensor(fin[:, b, :, :], ych[:, b, :, 0, :], ych[:, b, :, 1, :], ALU.add
                                ).then_inc(S["fin_pool"], 1)
                pool.wait_ge(S["fin_pool"], FIN_POOL.index(b) + 1)
                pool.wait_ge(S["yS_done"], 4)
                g.tensor_tensor(fin[:, b, :, :], fin[:, b, :, :], res[:, b, :, :], ALU.add).then_inc(fin_done[b], 1)

        @block.scalar
        def _(act):
            a = nc.scalar
            act.wait_ge(S["setup_pe"], 2)
            a.activation(wkT, bank[1][:, 0:4 * C].rearrange("p (c n) -> p c n", c=4), ACT.Copy
                         ).then_inc(S["setup_act"], 1)
            for q in range(2):
                act.wait_ge(S["setup_pe"], 4 + q)
                a.activation(a_sb[:, q, :, :], bank[4 + q][0:C, :].rearrange("p (c n) -> p c n", c=4), ACT.Copy
                             ).then_inc(S["setup_act"], 1)
            act.wait_ge(S["setup_pe"], 6)
            a.activation(wvT, bank[3][:, 0:4 * C].rearrange("p (c n) -> p c n", c=4), ACT.Copy
                         ).then_inc(S["setup_act"], 1)
            act.wait_ge(S["ld_small"], 80)
            a.activation(tg[:, :], gates[:, :], ACT.Tanh).then_inc(S["tg_done"], 1)
            a.add_instruction(mybir.InstLoadActFuncSet(name=nc.get_next_instruction_name(), act_func_set_id=6,
                                                       ins=[], outs=[]))
            def keep_scores_fold(h):
                act.wait_ge(S["fold_pe"], h + 1)
                a.activation(m_sb[:, :, h, :], bank[(0, 1, 6, 7)[h % 4]][:, :].rearrange("p (b k) -> p b k", b=B),
                             ACT.Copy).then_inc(S["fold_evac"], 1)

            keep_scores_fold(1)
            keep_scores_fold(3)
            act.wait_ge(S["mv1_done"], NT + 1)
            act.wait_ge(S["consts"], 1)
            a.activation(ln1[:, :, :], mv1[:, :, :, 1], ACT.Ln, bias=eps_c[:, 0:1]).then_inc(S["ln1_done"], 1)
            act.wait_ge(S["ln1_done"], 1)
            a.activation(y1[:, :, :], ln1[:, :, :], ACT.Exp, scale=-0.5).then_inc(S["y1_done"], 1)

            def keep_heads_fold(q):
                act.wait_ge(S["setup_pe"], 7 + q)
                a.activation(bvo_sb[:, q, :, :], bank[2 + q][0:C, :].rearrange("p (c n) -> p c n", c=4), ACT.Copy
                             ).then_inc(S["setup_act"], 1)

            def keep_values_fold(n):
                act.wait_ge(S["fold_pe"], HEADS + n + 1)
                for half in range(2):
                    ins = a.activation(vw_sb[64:128, n // 2 * 2 + half, :, :],
                                       bank[FOLD_BANK[n]][64 * half:64 * half + 64, :].rearrange(
                                           "p (c n) -> p c n", c=4), ACT.Copy)
                ins.then_inc(S["fold_evac"], 1)

            def high_halves(experts):
                for e in experts:
                    if e == 0:
                        act.wait_ge(S["ld_we"], 32)
                        act.wait_ge(S["xb_done"], B)
                    if (e + 1) * HE > sizes[0]:
                        act.wait_ge(S["scores_pe"], NT)
                    if (e + 1) * HE > sizes[0] + sizes[1]:
                        act.wait_ge(S["pv_pe"], NT)
                    a.activation(we1_hi[:, e, :], we1_sb[:, e, :], ACT.Copy).then_inc(S["we_hi"], 1)

            def normalise(b, par):
                since(act, b, 2, S["xnT_pe"], b - 1)
                for j in range(J):
                    a.activation(xn[:, par, j, :], pick(x_sb, b)[:, j, :], ACT.Identity,
                                 bias=pick(nb1, b)[:, j:j + 1], scale=pick(rs1, b)[:, j:j + 1]
                                 ).then_inc(S["xn_done"], 1)

            def keep_xnT(b, par):
                act.wait_ge(S["xnT_pe"], b + 1)
                since(act, b, 2, S["scores_pe"], (b - 1) * J)
                a.activation(xnT[:, par, :], bank[4][:, 0:J * P], ACT.Copy).then_inc(S["xnT_done"], 1)

            def exponent(s, j):
                act.wait_ge(S["shifted_done"], s * J + (j + 1))
                since(act, s, 1, S["norm_done"], s * J + (j - 1))
                a.activation(ex[:, j, :], shifted[:, j, :], ACT.Exp, scale=DH ** -0.5).then_inc(S["exp_done"], 1)

            def keep_prT(s, j):
                act.wait_ge(S["prT_pe"], s * J + (j + 1))
                since(act, s, 1, S["pv_pe"], s * J + (j - 1))
                a.activation(prT[:, j, :, :], bank[2 + j][:, :].rearrange("p (c n) -> p c n", c=4), ACT.Copy
                             ).then_inc(S["prT_done"], 1)

            keep_scores_fold(5)
            act.wait_ge(S["rs1_done"], 1)
            normalise(0, 0)
            keep_scores_fold(7)
            keep_xnT(0, 0)
            normalise(1, 1)

            def step(s, par):
                if on(s, 2):
                    act.wait_ge(S["x2T_pe"], s - 1)
                    a.activation(x2T_now[:, par, :], bank[5][:, 0:J * P], ACT.Copy).then_inc(S["x2T_done"], 1)
                if isinstance(s, int) and s == 0:
                    keep_xnT(1, 1)
                    keep_heads_fold(0)
                    keep_heads_fold(1)
                    exponent(0, 0)
                    exponent(0, 1)
                elif isinstance(s, int) and s == 1:
                    keep_values_fold(5)
                    exponent(1, 0)
                    exponent(1, 1)
                    keep_values_fold(7)
                    keep_xnT(2, 0)
                elif on(s, 0):
                    exponent(s, 0)
                    keep_xnT(s + 1, 1 - par)
                    exponent(s, 1)
                if on(s, 2):
                    a.activation(pick(x2T, s - 2), bank[5][:, 0:J * P], ACT.Copy).then_inc(S["x2T_kept"], 1)
                    if isinstance(s, int) and s >= B:
                        high_halves((0, 1, 2) if s == B else (5, 6))
                    act.wait_ge(S["gd_done"], s - 1)
                    a.activation(ge[:, :], gd[:, :], ACT.Exp, scale=1.0 / TAU).then_inc(S["ge_done"], 1)
                    if isinstance(s, int) and s >= B:
                        high_halves((3, 4) if s == B else ())
                if isinstance(s, int) and s == 0:
                    keep_values_fold(1)
                    keep_values_fold(3)
                if on(s, 0):
                    normalise(s + 2, par)
                if on(s, 1):
                    q = 1 - par
                    act.wait_ge(S["mv2_done"], s * J)
                    a.activation(ln2[:, :], mv2[:, :, 1], ACT.Ln, bias=eps_c[:, 0:1]).then_inc(S["ln2_done"], 1)
                    act.wait_ge(S["ln2_done"], s)
                    a.activation(y2[:, :], ln2[:, :], ACT.Exp, scale=-0.5).then_inc(S["y2_done"], 1)
                if on(s, 0):
                    keep_prT(s, 0)
                    keep_prT(s, 1)
                if on(s, 1):
                    act.wait_ge(S["rs2_done"], s)
                    since(act, s, 3, scat[q], (s - (1 + q)) * (16 * J))
                    for j in range(J):
                        a.activation(payload[:, q, j, :, 0:D], x1[:, q, j, :].unsqueeze(1).to_broadcast([P, 2, D]),
                                     ACT.Identity, bias=nb2[:, j:j + 1], scale=ln2r[:, j:j + 1]
                                     ).then_inc(S["pay_x"], 1)

            steps(act, step)

            act.wait_ge(S["ld_b3"], 32)
            for c in range(4):
                for m in range(SC):
                    n = SC * c + m
                    act.wait_ge(S["up_pe"], n + 1)
                    if n >= 2:
                        act.wait_ge(S["hidS_done"], n - 1)
                    a.activation(gel[:, m, :], bank[m][:, :], ACT.Gelu, bias=bs1_sb[:, SC + m:SC + m + 1]
                                 ).then_inc(S["gel_done"], 1)
                high_halves(((7, 8), (9, 10), (11,), ())[c])
            U0 = 4 * SC

            def keep_tokT(k, par):
                act.wait_ge(S["tokT_pe"], k + 1)
                act.wait_ge(S["up_pe"], k + (U0 - 1))
                a.activation(tokT[:, par, 0, :], bank[5 + 2 * par][:, 0:P], ACT.Copy).then_inc(S["tokT_hi"], 1)

            def tile(i, u):
                par = u % 2
                if on(i, -1, TILES):
                    keep_tokT(i + 1, 1 - par)
                if on(i, 0, TILES):
                    act.wait_ge(S["up_pe"], i + (U0 + 1))
                    if isinstance(i, int) and i < 2:
                        act.wait_ge(S["hidS_done"], U0)
                    else:
                        act.wait_ge(S["hid_done"], i - 1)
                    a.activation(gel[:, par, 0:HR], bank[par][:, 0:HR], ACT.Gelu).then_inc(S["gel_done"], 1)
                if on(i, 2, TILES):
                    v = (u - 2) % 4
                    act.wait_ge(S["y_pe"], i - 1)
                    act.wait_ge(S["meta_done"], i - 1)
                    since(act, i, 6, tile_out[v], (i - (2 + v)) * 4)
                    a.activation(yt[:, v, :], bank[4][:, 0:D], ACT.Copy, scale=meta[:, v, 0:1]
                                 ).then_inc(S["yt_done"], 1)

            keep_tokT(0, 0)
            tile_steps(act, tile)

        @block.vector
        def _(dve):
            v = nc.vector
            dve.wait_ge(S["setup_pe"], 1)
            v.tensor_copy(wqT, bank[0][:, :].rearrange("p (c n) -> p c n", c=4)).then_inc(S["setup_dve"], 1)
            dve.wait_ge(S["setup_pe"], 3)
            v.tensor_copy(ctxT, bank[2][0:C, :]).then_inc(S["setup_dve"], 1)
            v.memset(mv1[:, B:B + 2, :, :], 0.0).then_inc(S["mv1_done"], 1)
            dve.wait_ge(S["ld_x"], 16)
            for t in range(NT):
                v.bn_stats(st1[:, t, :], x_sb[:, t // J, t % J, :]).then_inc(S["st1_done"], 1)
            def keep_scores_fold(h):
                dve.wait_ge(S["fold_pe"], h + 1)
                v.tensor_copy(m_sb[:, :, h, :], bank[(0, 1, 6, 7)[h % 4]][:, :].rearrange("p (b k) -> p b k", b=B)
                              ).then_inc(S["fold_evac_dve"], 1)

            keep_scores_fold(0)
            dve.wait_ge(S["st1_done"], NT)
            for t in range(NT):
                v.bn_aggr(mv1[:, t // J, t % J, :], st1[:, t, :]).then_inc(S["mv1_done"], 1)

            dve.wait_ge(S["ld_mask"], 16)
            v.tensor_scalar(mask_add[:, :, :], mask_sb[:, :, :], 0.0, MASKED, ALU.is_equal, ALU.mult
                            ).then_inc(S["mask_done"], 1)
            keep_scores_fold(2)
            dve.wait_ge(S["y1_done"], 1)
            v.tensor_tensor(q1[:, 0, :, :], y1[:, :, :], y1[:, :, :], ALU.mult).then_inc(S["newton1"], 1)
            dve.wait_ge(S["newton1"], 1)
            v.scalar_tensor_tensor(out=q1[:, 1, :, :], in0=mv1[:, :, :, 1], scalar=EPS, in1=q1[:, 0, :, :],
                                   op0=ALU.add, op1=ALU.mult).then_inc(S["newton1"], 1)
            dve.wait_ge(S["newton1"], 2)
            v.tensor_scalar(q1[:, 2, :, :], q1[:, 1, :, :], -0.5, 1.5, ALU.mult, ALU.add).then_inc(S["newton1"], 1)
            dve.wait_ge(S["newton1"], 3)
            v.tensor_tensor(rs1[:, :, :], y1[:, :, :], q1[:, 2, :, :], ALU.mult).then_inc(S["newton1"], 1)
            dve.wait_ge(S["newton1"], 4)
            v.scalar_tensor_tensor(out=nb1[:, :, :], in0=mv1[:, :, :, 0], scalar=-1.0, in1=rs1[:, :, :], op0=ALU.mult,
                                   op1=ALU.mult).then_inc(S["rs1_done"], 1)
            for h in range(4, HEADS, 2):
                keep_scores_fold(h)

            def keep_values_fold(n):
                dve.wait_ge(S["fold_pe"], HEADS + n + 1)
                for half in range(2):
                    ins = v.tensor_copy(vw_sb[0:64, n // 2 * 2 + half, :, :],
                                        bank[FOLD_BANK[n]][64 * half:64 * half + 64, :].rearrange(
                                            "p (c n) -> p c n", c=4))
                ins.then_inc(S["fold_evac_dve"], 1)

            def split_biases():
                dve.wait_ge(S["ld_be"], 32)
                for dst, lo in ((b1_raw, 0), (b2_raw[:, :], HE)):
                    w = HE if lo == 0 else D
                    v.tensor_copy(b_parts[:, 0, lo:lo + w], dst).then_inc(S["bias_rest"], 1)
                dve.wait_ge(S["bias_rest"], 2)
                for dst, lo in ((b1_raw, 0), (b2_raw[:, :], HE)):
                    w = HE if lo == 0 else D
                    v.tensor_tensor(b_rest[:, 0, lo:lo + w], dst, b_parts[:, 0, lo:lo + w], ALU.subtract
                                    ).then_inc(S["bias_rest"], 1)
                dve.wait_ge(S["bias_rest"], 4)
                v.tensor_copy(b_parts[:, 1, :], b_rest[:, 0, :]).then_inc(S["bias_parts"], 1)
                dve.wait_ge(S["bias_parts"], 1)
                v.tensor_tensor(b_rest[:, 1, :], b_rest[:, 0, :], b_parts[:, 1, :], ALU.subtract
                                ).then_inc(S["bias_parts"], 1)
                dve.wait_ge(S["bias_parts"], 2)
                v.tensor_copy(b_parts[:, 2, :], b_rest[:, 1, :]).then_inc(S["bias_parts"], 1)

            def step(s, par):
                now, one, two = on(s, 0), on(s, 1), on(s, 2)
                if isinstance(s, int) and s == B:
                    split_biases()
                n = s - 1
                q = 1 - par
                if now:
                    sc = [bank[j][:, :].rearrange("p (h k) -> p h k", h=HEADS) for j in range(J)]
                    for j in range(J):
                        dve.wait_ge(S["scores_pe"], s * J + (j + 1))
                        v.tensor_reduce(smax[:, par, j, :], sc[j], AX.X, ALU.max).then_inc(S["smax_done"], 1)
                    for j in range(J):
                        dve.wait_ge(S["smax_done"], s * J + (j + 1))
                        since(dve, s, 1, S["exp_done"], s * J + (j - 1))
                        v.tensor_tensor(shifted[:, j, :].rearrange("p (h k) -> p h k", h=HEADS), sc[j],
                                        smax[:, par, j, :].unsqueeze(2).to_broadcast([P, HEADS, KEYS]), ALU.subtract
                                        ).then_inc(S["shifted_done"], 1)

                if isinstance(s, int) and s == 1:
                    keep_values_fold(4)

                def sum_exp(j):
                    dve.wait_ge(S["exp_done"], s * J + (j + 1))
                    v.tensor_reduce(ssum[:, par, j, :], ex[:, j, :].rearrange("p (h k) -> p h k", h=HEADS),
                                    AX.X, ALU.add).then_inc(S["ssum_done"], 1)

                def invert_sum(j):
                    dve.wait_ge(S["ssum_done"], s * J + (j + 1))
                    v.reciprocal(srec[:, par, j, :], ssum[:, par, j, :]).then_inc(S["srec_done"], 1)

                if two:
                    dve.wait_ge(S["logits_pe"], n)
                    v.tensor_tensor(lg[:, :, :], bank[7][:, 0:J * E].rearrange("p (j e) -> p j e", j=J),
                                    br_sb[:, :].unsqueeze(1).to_broadcast([P, J, E]), ALU.add).then_inc(S["lg_done"], 1)
                if now:
                    sum_exp(0)
                if two:
                    apart(dve, (S["lg_done"], n))
                    for j in range(J):
                        v.max(top[:, j, :], lg[:, j, :]).then_inc(S["top_done"], 1)
                if now:
                    invert_sum(0)
                    sum_exp(1)
                if two:
                    apart(dve, (S["top_done"], n * J))
                    for j in range(J):
                        v.max_index(topi[:, j, :], top[:, j, :], lg[:, j, :]).then_inc(S["topi_done"], 1)
                    v.tensor_tensor(gd[:, :], top[:, :, 1], top[:, :, 0], ALU.subtract).then_inc(S["gd_done"], 1)
                if now:
                    invert_sum(1)
                if isinstance(s, int) and s == 0:
                    keep_values_fold(0)
                    keep_values_fold(2)
                if isinstance(s, int) and s == 1:
                    keep_values_fold(6)
                if one:
                    dve.wait_ge(S["pv_pe"], s * J)
                    since(dve, s, 3, S["res0_done"], s - 2)
                    if isinstance(s, int) and s == 1:
                        dve.wait_ge(S["xb_done"], B)
                    v.scalar_tensor_tensor(out=x1[:, q, :, :].rearrange("p j d -> p (j d)"), in0=bank[6][:, 0:J * D],
                                           scalar=tg[:, 0:1], in1=pick(xb, s - 1).rearrange("p j d -> p (j d)"),
                                           op0=ALU.mult, op1=ALU.add).then_inc(S["x1_done"], 1)
                if two:
                    dve.wait_ge(S["topi_done"], n * J)
                    v.tensor_copy(topf[:, :, :], topi[:, :, 0:2]).then_inc(S["topf_done"], 1)
                if one:
                    dve.wait_ge(S["x1_done"], s)
                    v.bn_stats(st2[:, 0, :], x1[:, q, 0, :]).then_inc(S["st2_done"], 1)
                if two:
                    dve.wait_ge(S["topf_done"], n)
                    v.tensor_tensor(oh[:, :, :, :],
                                    iota_e[:, :].unsqueeze(1).unsqueeze(1).to_broadcast([P, J, 2, E]),
                                    topf[:, :, :].unsqueeze(3).to_broadcast([P, J, 2, E]), ALU.is_equal
                                    ).then_inc(S["oh_done"], 1)
                if one:
                    v.bn_stats(st2[:, 1, :], x1[:, q, 1, :]).then_inc(S["st2_done"], 1)
                if two:
                    dve.wait_ge(S["oh_done"], n)
                    v.tensor_tensor(hot[:, par, :, :], oh[:, :, 0, :], oh[:, :, 1, :], ALU.add
                                    ).then_inc(S["hot_done"], 1)
                if one:
                    apart(dve, (S["st2_done"], s * J))
                    for j in range(J):
                        v.bn_aggr(mv2[:, j, :], st2[:, j, :]).then_inc(S["mv2_done"], 1)
                if two:
                    dve.wait_ge(S["hot_done"], n)
                    v.tensor_tensor(seen_j[:, :], pick(seen, s - 2), hot[:, par, 0, :], ALU.add
                                    ).then_inc(S["seenj_done"], 1)
                if two:
                    dve.wait_ge(S["ge_done"], n)
                    v.tensor_scalar(gz[:, :], ge[:, :], 1.0, None, ALU.add).then_inc(S["gz_done"], 1)
                if two:
                    dve.wait_ge(S["seenj_done"], n)
                    v.tensor_tensor(pick(seen, s - 1), seen_j[:, :], hot[:, par, 1, :], ALU.add
                                    ).then_inc(S["seen_done"], 1)
                if two:
                    dve.wait_ge(S["pos_pe"], n)
                    v.tensor_tensor(pb[:, :, :], bank[7][:, 32:32 + J * E].rearrange("p (j e) -> p j e", j=J),
                                    base_e[:, :].unsqueeze(1).to_broadcast([P, J, E]), ALU.add
                                    ).then_inc(S["pb_done"], 1)
                if one:
                    dve.wait_ge(S["y2_done"], s)
                    v.tensor_tensor(q2[:, :], y2[:, :], y2[:, :], ALU.mult).then_inc(S["q2a"], 1)
                if two:
                    dve.wait_ge(S["gz_done"], n)
                    v.reciprocal(gr[:, :], gz[:, :]).then_inc(S["gz2_done"], 1)
                if one:
                    dve.wait_ge(S["q2a"], s)
                    v.scalar_tensor_tensor(out=rs2[:, 0, :], in0=mv2[:, :, 1], scalar=EPS, in1=q2[:, :], op0=ALU.add,
                                           op1=ALU.mult).then_inc(S["q2b"], 1)
                if two:
                    dve.wait_ge(S["pb_done"], n)
                    v.tensor_tensor(sl[:, :, :, :], oh[:, :, :, :], pb[:, :, :].unsqueeze(2).to_broadcast([P, J, 2, E]),
                                    ALU.mult).then_inc(S["sl_done"], 1)
                if one:
                    dve.wait_ge(S["q2b"], s)
                    v.tensor_scalar(rs2[:, 1, :], rs2[:, 0, :], -0.5, 1.5, ALU.mult, ALU.add).then_inc(S["q2c"], 1)
                if two:
                    dve.wait_ge(S["gz2_done"], n)
                    since(dve, s, 4, scat[par], (s - (2 + par)) * (16 * J))
                    v.tensor_scalar(payload[:, par, :, 0, D:D + 1].rearrange("p j o -> p (j o)"), gr[:, :], tg[:, 1:2],
                                    None, ALU.mult).then_inc(S["gr_done"], 1)
                if one:
                    dve.wait_ge(S["q2c"], s)
                    since(dve, s, 2, S["pay_x"], (s - 1) * J)
                    v.tensor_tensor(ln2r[:, :], y2[:, :], rs2[:, 1, :], ALU.mult).then_inc(S["q2d"], 1)
                if two:
                    v.scalar_tensor_tensor(out=payload[:, par, :, 1, D:D + 1].rearrange("p j o -> p (j o)"),
                                           in0=gr[:, :], scalar=tg[:, 1:2], in1=ge[:, :], op0=ALU.mult,
                                           op1=ALU.mult).then_inc(S["gr_done"], 1)
                if one:
                    dve.wait_ge(S["q2d"], s)
                    v.scalar_tensor_tensor(out=nb2[:, :], in0=mv2[:, :, 0], scalar=-1.0, in1=ln2r[:, :], op0=ALU.mult,
                                           op1=ALU.mult).then_inc(S["rs2_done"], 1)
                if two:
                    dve.wait_ge(S["sl_done"], n)
                    v.tensor_reduce(slot_f[:, :, :], sl[:, :, :, :], AX.X, ALU.add).then_inc(S["slotf_done"], 1)
                    dve.wait_ge(S["slotf_done"], n)
                    v.tensor_copy(slot_i[:, par, :, :], slot_f[:, :, :]).then_inc(S["slot_done"], 1)

            steps(dve, step)

            def keep_tokT(k, par):
                dve.wait_ge(S["tokT_hi"], k + 1)
                v.tensor_tensor(tokT[:, par, 1, :], bank[5 + 2 * par][:, 0:P], tokT[:, par, 0, :].bitcast(F32),
                                ALU.subtract).then_inc(S["tokT_done"], 1)

            def low_halves(e):
                dve.wait_ge(S["we_hi"], e + 1)
                v.tensor_tensor(we1_lo[:, e, :], we1_sb[:, e, :], we1_hi[:, e, :].bitcast(F32), ALU.subtract
                                ).then_inc(S["we_lo_dve"], 1)

            def shared_hidden(c):
                for m in range(SC):
                    n = SC * c + m
                    dve.wait_ge(S["gel_done"], n + 1)
                    if c >= 2:
                        dve.wait_ge(S["yS_pe"], c - 1)
                    v.scalar_tensor_tensor(out=hid_s[c % 2][:, m, :], in0=bank[2 + m][:, :], scalar=bs1_sb[:, m:m + 1],
                                           in1=gel[:, m, :], op0=ALU.add, op1=ALU.mult).then_inc(S["hidS_done"], 1)
                    if c == 3 and m == 0:
                        low_halves(10)

            links = [1]

            def link(ins):
                links[0] += 1
                ins.then_inc(S["chain_dve"], 1)
                dve.wait_ge(S["chain_dve"], links[0] - 1)

            dve.wait_ge(S["cnt_pe"], 1)
            link(v.tensor_copy(cnt[:, :], bank[7][0:1, 64:64 + E]))
            v.tensor_tensor(pad_i[:, :], cnt[:, :], base_e[0:1, :], ALU.add).then_inc(S["pad_ready"], 1)
            shared_hidden(0)
            link(v.tensor_scalar(til[:, :], cnt[:, :], float(P - 1), None, ALU.add))
            link(v.tensor_copy(cnt_i[:, 0, :], til[:, :]))
            link(v.tensor_scalar(cnt_i[:, 1, :], cnt_i[:, 0, :], 7, None, ALU.logical_shift_right))
            link(v.tensor_copy(til[:, :], cnt_i[:, 1, :]))
            link(v.tensor_tensor(tt[:, :, :], tri_e[:, :, :], til[:, :].unsqueeze(1).to_broadcast([1, E, E]), ALU.mult))
            link(v.tensor_reduce(cum[:, :], tt[:, :, :], AX.X, ALU.add))
            link(v.tensor_scalar(coef[:, :], til[:, :], -float(P), float(CAP), ALU.mult, ALU.add))
            for c in range(4):
                if c < 3:
                    shared_hidden(c + 1)
                else:
                    keep_tokT(0, 0)
                dve.wait_ge(S["yS_pe"], c + 1)
                if c == 0:
                    dve.wait_ge(S["res0_done"], B)
                o = res[:, 2 * c:2 * c + 2, :, :].rearrange("p b j d -> p (b j d)")
                v.scalar_tensor_tensor(out=o, in0=bank[4 + 2 * (c % 2)][:, :], scalar=tg[:, 1:2], in1=o,
                                       op0=ALU.mult, op1=ALU.add).then_inc(S["yS_done"], 1)
                if c == 0:
                    link(v.tensor_tensor(ind[:, :, :], cum[:, :].unsqueeze(1).to_broadcast([1, TILES, E]),
                                         tile_no[:, :].unsqueeze(2).to_broadcast([1, TILES, E]), ALU.is_le))
                    link(v.tensor_reduce(exp_f[:, :], ind[:, :, :], AX.X, ALU.add))
                    v.tensor_scalar(exp_i[:, :], exp_f[:, :], float(E - 1), None, ALU.min).then_inc(S["table_done"], 1)
                    link(v.tensor_tensor(indc[:, :, :], ind[:, :, :], coef[:, :].unsqueeze(1).to_broadcast([1, TILES, E]),
                                         ALU.mult))
                    link(v.tensor_reduce(row_s[:, :], indc[:, :, :], AX.X, ALU.add))
                    link(v.scalar_tensor_tensor(out=row_f[:, :], in0=tile_no[:, :], scalar=float(P), in1=row_s[:, :],
                                                op0=ALU.mult, op1=ALU.add))
                    v.tensor_scalar(row_i[:, :], row_f[:, :], float(E * CAP), None, ALU.min
                                    ).then_inc(S["table_done"], 1)
                for e in ((), (8, 9), (11,), ())[c]:
                    low_halves(e)
            U0 = 4 * SC

            def tile(i, u):
                par = u % 2
                if on(i, -1, TILES):
                    keep_tokT(i + 1, 1 - par)
                if on(i, 1, TILES):
                    dve.wait_ge(S["hidT_pe"], i)
                    since(dve, i, 3, S["y_pe"], i - 2)
                    v.tensor_copy(hidT[:, 1 - par, :], bank[6][:, 0:HR]).then_inc(S["hidT_done"], 1)
                if on(i, 0, TILES):
                    dve.wait_ge(S["gel_done"], i + (U0 + 1))
                    since(dve, i, 2, S["hidT_pe"], i - 1)
                    v.tensor_tensor(hid[:, par, :], bank[2 + par][:, 0:HR], gel[:, par, 0:HR], ALU.mult
                                    ).then_inc(S["hid_done"], 1)

            tile_steps(dve, tile)

            for b in FIN_VECTOR:
                dve.wait_ge(ych_in[b], 16)
                v.tensor_tensor(fin[:, b, :, :], ych[:, b, :, 0, :], ych[:, b, :, 1, :], ALU.add
                                ).then_inc(S["fin_a"], 1)
                dve.wait_ge(S["fin_a"], FIN_VECTOR.index(b) + 1)
                v.tensor_tensor(fin[:, b, :, :], fin[:, b, :, :], res[:, b, :, :], ALU.add).then_inc(fin_done[b], 1)

        @block.tensor
        def _(pe):
            t = nc.tensor
            def stay_warm(count, b):
                for _ in range(count):
                    t.matmul(bank[b][:, :], ones_b[:, :], ones_b[:, :].unsqueeze(1).to_broadcast([P, 4, P]),
                             start=True, stop=True)

            pe.wait_ge(S["ones_set"], 1)
            stay_warm(8, 7)
            pe.wait_ge(S["consts"], 1)
            pe.wait_ge(S["ld_wq"], 16)
            for c in range(4):
                ins = t.transpose(bank[0][:, c * P:(c + 1) * P], wq_sb[:, c, :], ident[:, :])
            ins.then_inc(S["setup_pe"], 1)
            pe.wait_ge(S["ld_wk"], 16)
            for c in range(4):
                ins = t.transpose(bank[1][:, c * C:(c + 1) * C], wk_sb[:, c, :], ident[0:C, 0:C])
            ins.then_inc(S["setup_pe"], 1)
            pe.wait_ge(S["ld_ctx"], 16)
            for c in range(4):
                ins = t.transpose(bank[2][0:C, c * P:(c + 1) * P], ctx_sb[:, c, :], ident[:, :])
            ins.then_inc(S["setup_pe"], 1)
            pe.wait_ge(S["setup_dve"], 1)
            pe.wait_ge(S["setup_act"], 1)
            for q in range(2):
                for c in range(4):
                    ins = t.matmul(bank[4 + q][0:C, c * P:(c + 1) * P], wkT[64 * q:64 * q + 64, c, :],
                                   wqT[64 * q:64 * q + 64, c, :], start=True, stop=True)
                ins.then_inc(S["setup_pe"], 1)
            pe.wait_ge(S["ld_wv"], 16)
            for c in range(4):
                ins = t.transpose(bank[3][:, c * C:(c + 1) * C], wv_sb[:, c, :], ident[0:C, 0:C])
            ins.then_inc(S["setup_pe"], 1)

            def fold_scores(h):
                if h >= 4:
                    pe.wait_ge(S["fold_evac_dve"] if h % 2 == 0 else S["fold_evac"], (h - 4) // 2 + 1)
                t.matmul(bank[(0, 1, 6, 7)[h % 4]][:, :], a_sb[:, h % 2, h // 2, :], ctxT, start=True, stop=True
                         ).then_inc(S["fold_pe"], 1)

            def fold_heads():
                pe.wait_ge(S["ld_wo"], 16)
                pe.wait_ge(S["setup_act"], 4)
                for q in range(2):
                    for c in range(4):
                        ins = t.matmul(bank[2 + q][0:C, c * P:(c + 1) * P], wvT[64 * q:64 * q + 64, c, :],
                                       wo_sb[64 * q:64 * q + 64, c, :], start=True, stop=True)
                    ins.then_inc(S["setup_pe"], 1)

            def fold_values(n):
                if n >= 5:
                    pe.wait_ge(S["fold_evac_dve"] if n % 2 == 0 else S["fold_evac"], {5: 5, 6: 7, 7: 7}[n])
                t.matmul(bank[FOLD_BANK[n]][:, :], ctxT[:, n // 2 * P:(n // 2 + 1) * P],
                         bvo_sb[:, n % 2, :, :].rearrange("p c n -> p (c n)"), start=True, stop=True
                         ).then_inc(S["fold_pe"], 1)

            def turn_xn(b, par):
                pe.wait_ge(S["xn_done"], b * J + J)
                for j in range(J):
                    ins = t.transpose(bank[4][:, j * P:(j + 1) * P], xn[:, par, j, :], ident[:, :])
                ins.then_inc(S["xnT_pe"], 1)

            def turn_pr(s, j):
                pe.wait_ge(S["norm_done"], (s - 1) * J + (j + 1))
                for c in range(4):
                    ins = t.transpose(bank[2 + j][:, c * P:(c + 1) * P], pr[:, j, c * P:(c + 1) * P], ident[:, :])
                ins.then_inc(S["prT_pe"], 1)

            def attend(s, j):
                if j == 0:
                    since(pe, s, 2, S["x1_done"], s - 1)
                pe.wait_ge(S["prT_done"], (s - 1) * J + (j + 1))
                for c in range(4):
                    ins = t.matmul(bank[6][:, j * D:(j + 1) * D], prT[:, j, c, :], pick(vw_sb, s - 1)[:, c, :],
                                   start=(c == 0), stop=(c == 3))
                ins.then_inc(S["pv_pe"], 1)

            def score(s, par, j):
                since(pe, s, 1, S["shifted_done"], s * J + (j - 1))
                t.matmul(bank[j][:, :], xnT[:, par, j * P:(j + 1) * P],
                         pick(m_sb, s).rearrange("p h k -> p (h k)"), start=True, stop=False)
                t.matmul(bank[j][:, :], one_row[:, :],
                         pick(mask_add, s).unsqueeze(1).to_broadcast([1, HEADS, KEYS]), start=False, stop=True
                         ).then_inc(S["scores_pe"], 1)

            def rank(s, par):
                n = s - 2
                sv = pick(seen, s - 3)
                pe.wait_ge(S["lg_done"], n)
                pe.wait_ge(S["hot_done"], n)
                t.matmul(bank[7][:, 32:32 + E], ones_b[:, :], sv, start=True, stop=False)
                t.matmul(bank[7][:, 32:32 + E], before[:, :], hot[:, 1 - par, 0, :], start=False, stop=True)
                t.matmul(bank[7][:, 32 + E:32 + 2 * E], ones_b[:, :], sv, start=True, stop=False)
                t.matmul(bank[7][:, 32 + E:32 + 2 * E], ones_b[:, :], hot[:, 1 - par, 0, :], start=False, stop=False)
                t.matmul(bank[7][:, 32 + E:32 + 2 * E], before[:, :], hot[:, 1 - par, 1, :], start=False, stop=True
                         ).then_inc(S["pos_pe"], 1)

            def turn_tokens(k, u):
                pe.wait_ge(tile_in[u], (k - u) * 4 + 16)
                t.transpose(bank[5 + 2 * (u % 2)][:, 0:P], tok[:, u, 0:D], ident[:, :]).then_inc(S["tokT_pe"], 1)

            def shared_up(c, halves=range(SC)):
                for m in halves:
                    n = SC * c + m
                    if n >= 2:
                        pe.wait_ge(S["hidS_done"], n - 1)
                    xt = x2T[:, 2 * c:2 * c + 2, :].rearrange("p b n -> p (b n)")
                    t.matmul(bank[m][:, :], ws1_sb[:, (SC + m) * P:(SC + m + 1) * P], xt, start=True, stop=True)
                    t.matmul(bank[2 + m][:, :], ws1_sb[:, m * P:(m + 1) * P], xt, start=True, stop=True
                             ).then_inc(S["up_pe"], 1)

            def step(s, par):
                if on(s, 0):
                    pe.wait_ge(S["xnT_done"], s + 1)
                    score(s, par, 0)
                    score(s, par, 1)
                if isinstance(s, int) and s == 2:
                    pe.wait_ge(S["fold_evac_dve"], 8)
                    pe.wait_ge(S["fold_evac"], 8)
                if isinstance(s, int) and s == 1:
                    pe.wait_ge(S["fold_evac_dve"], 6)
                    pe.wait_ge(S["fold_evac"], 6)
                if on(s, 1):
                    turn_pr(s, 0)
                if on(s, 3):
                    rank(s, par)
                if isinstance(s, int) and s == B + 1:
                    shared_up(0, (1,))
                if on(s, 1):
                    turn_pr(s, 1)
                if isinstance(s, int) and s == 1:
                    for n in range(4, 8):
                        fold_values(n)
                if on(s, 1):
                    attend(s, 0)
                if on(s, 2):
                    n = s - 1
                    pe.wait_ge(S["pay_x"], n * J)
                    since(pe, s, 3, S["x2T_kept"], n - 1)
                    for j in range(J):
                        ins = t.transpose(bank[5][:, j * P:(j + 1) * P], payload[:, par, j, 0, 0:D], ident[:, :])
                    ins.then_inc(S["x2T_pe"], 1)
                if on(s, 0):
                    turn_xn(s + 1, 1 - par)
                if isinstance(s, int) and s == 0:
                    fold_heads()
                    pe.wait_ge(S["setup_act"], 6)
                    for n in range(4):
                        fold_values(n)
                if on(s, 1):
                    attend(s, 1)
                if on(s, 2):
                    pe.wait_ge(S["x2T_done"], n)
                    since(pe, s, 3, S["pb_done"], n - 1)
                    for j in range(J):
                        ins = t.matmul(bank[7][:, j * E:(j + 1) * E], x2T_now[:, par, j * P:(j + 1) * P], wr_sb[:, :],
                                       start=True, stop=True)
                    ins.then_inc(S["logits_pe"], 1)
                if isinstance(s, int) and s == B:
                    pe.wait_ge(S["ld_ws"], 48)
                    pe.wait_ge(S["x2T_kept"], 2)
                    pe.wait_ge(S["shifted_done"], NT)
                    pe.wait_ge(S["prT_done"], NT)
                    shared_up(0, (0,))
                if isinstance(s, int) and s == B + 1:
                    stay_warm(5, 4)

            pe.wait_ge(S["setup_dve"], 2)
            pe.wait_ge(S["setup_act"], 3)
            for h in range(HEADS):
                fold_scores(h)
            turn_xn(0, 0)
            pe.wait_ge(S["fold_evac_dve"], 4)
            pe.wait_ge(S["fold_evac"], 4)
            pe.wait_ge(S["mask_done"], 1)
            pe.wait_ge(S["ld_wr"], 16)

            steps(pe, step)
            rank(B + 2, 0)

            pe.wait_ge(S["seen_done"], B)
            pe.wait_ge(S["pb_done"], B)
            t.matmul(bank[7][:, 64:64 + E], ones_b[:, :], seen[:, B, :], start=True, stop=True).then_inc(S["cnt_pe"], 1)
            stay_warm(8, 4)

            pe.wait_ge(S["x2T_kept"], B)
            for c in range(4):
                if c < 3:
                    shared_up(c + 1)
                else:
                    turn_tokens(0, 0)
                pe.wait_ge(S["hidS_done"], SC * (c + 1))
                if c >= 2:
                    pe.wait_ge(S["yS_done"], c - 1)
                for n in range(4):
                    for m in range(SC):
                        ins = t.matmul(bank[4 + 2 * (c % 2)][:, n * D:(n + 1) * D],
                                       hid_s[c % 2][:, m, n * P:(n + 1) * P], ws2_sb[:, m, :],
                                       start=(m == 0), stop=(m == SC - 1))
                ins.then_inc(S["yS_pe"], 1)

            pe.wait_ge(S["ld_we"], 32)
            pe.wait_ge(S["we_lo_pool"], 8)
            pe.wait_ge(S["we_lo_dve"], 4)
            pe.wait_ge(S["table_done"], 2)
            pe.wait_ge(S["chain_dve"], 1)
            pe.wait_ge(S["hidS_done"], 4 * SC)

            def expert_of(k):
                return nc.values_load(exp_i[0:1, bass.ds(k, 1)], engines=(mybir.EngineType.PE,), min_val=0,
                                      max_val=E - 1, skip_runtime_bounds_check_because="a count, cut at E - 1")

            def tile(i, u):
                par = u % 2
                if on(i, 0, TILES):
                    e_up = expert_of(i)
                if on(i, -1, TILES):
                    turn_tokens(i + 1, (u + 1) % 4)
                if on(i, 0, TILES):
                    w_hi, w_lo = pick(we1_hi, e_up), pick(we1_lo, e_up)
                    bias = pick(b1_3, e_up)
                    pe.wait_ge(S["tokT_done"], i + 1)

                    def up(out, cols):
                        t.matmul(out, tokT[:, par, 0, :], w_hi[:, cols], start=True, stop=False)
                        t.matmul(out, tokT[:, par, 0, :], w_lo[:, cols], start=False, stop=False)
                        t.matmul(out, tokT[:, par, 1, :], w_hi[:, cols], start=False, stop=False)

                    up(bank[par][:, 0:HR], slice(HR, HE))
                    t.matmul(bank[par][:, 0:HR], three_rows[:, :], bias[0:3, HR:HE], start=False, stop=True)
                    up(bank[2 + par][:, 0:HR], slice(0, HR))
                if on(i, 2, TILES):
                    e_down = expert_of(i - 2)
                if on(i, 0, TILES):
                    t.matmul(bank[2 + par][:, 0:HR], three_rows[:, :], bias[0:3, 0:HR], start=False, stop=True
                             ).then_inc(S["up_pe"], 1)
                if on(i, 2, TILES):
                    w = pick(we2_sb, e_down)
                    pe.wait_ge(S["hidT_done"], i - 1)
                    since(pe, i, 3, S["yt_done"], i - 2)
                    for c in range(RC):
                        t.matmul(bank[4][:, 0:D], hidT[:, par, c * P:(c + 1) * P], w[:, c, :], start=(c == 0),
                                 stop=False)
                    t.matmul(bank[4][:, 0:D], three_rows[:, :], pick(b2_3, e_down)[0:3, :], start=False, stop=True
                             ).then_inc(S["y_pe"], 1)
                if on(i, 1, TILES):
                    pe.wait_ge(S["hid_done"], i)
                    if isinstance(i, int) and i == 1:
                        pe.wait_ge(S["yS_done"], 4)
                    for c in range(RC):
                        ins = t.transpose(bank[6][:, c * P:(c + 1) * P], hid[:, 1 - par, c * P:(c + 1) * P],
                                          ident[:, :])
                    ins.then_inc(S["hidT_pe"], 1)

            tile_steps(pe, tile)


_INS = ["x", "ctx_768", "mask_BxS2_bk0", "g_xattn", "g_ffn", "L0_xattn_W_q", "L0_xattn_W_k", "L0_xattn_W_v",
        "L0_xattn_W_o", "L0_xattn_b_o", "L0_ffn_Ws1", "L0_ffn_bs1", "L0_ffn_Ws2", "L0_ffn_bs2", "L0_ffn_We1",
        "L0_ffn_be1", "L0_ffn_We2", "L0_ffn_be2", "L0_ffn_Wr", "L0_ffn_br"]


def kernel(**inputs):
    import numpy as np
    import concourse.bacc as bacc
    from concourse.bass_utils import run_bass_kernel_spmd

    nc = bacc.Bacc("TRN2", target_bir_lowering=False, num_devices=1)
    arrays, args = {}, []
    for name in _INS:
        a = np.ascontiguousarray(inputs[name])
        arrays[f"in_{name}"] = a
        args.append(nc.dram_tensor(f"in_{name}", a.shape, mybir.dt.from_np(a.dtype), kind="ExternalInput").ap())
    shape = inputs["x"].shape
    out = nc.dram_tensor("out_dram", shape, F32, kind="ExternalOutput").ap()
    flamingo_block(nc, *args, out)
    return run_bass_kernel_spmd(nc, [arrays], core_ids=[0]).results[0]["out_dram"]
```
